# Optimizing a Trainium2 kernel written in Bass

```python
import numpy as np
import jax
import jax.numpy as jnp

def _softmax(x, axis=-1):
    return jax.nn.softmax(x, axis=axis)

def _gelu(x):
    return jax.nn.gelu(x, approximate=True)

def _silu(x):
    return jax.nn.silu(x)

def _sigmoid(x):
    return jax.nn.sigmoid(x)

def _layernorm(x, axis=-1, eps=1e-05):
    m = jnp.mean(x, axis=axis, keepdims=True)
    v = jnp.var(x, axis=axis, keepdims=True)
    return (x - m) / jnp.sqrt(v + eps)

def _scatter_add(tgt, idx, src, axis=0):
    return tgt.at[idx].add(src)

def _segment_sum(src, seg, n):
    return jax.ops.segment_sum(src, seg, n)
kernel_name = 'mk_gnn_preln_d4_gnn_r16_1c521f'

def setup_inputs(seed: int=0):
    np.random.seed(seed)
    _w = jnp.asarray

    def _rec_inputs():
        import jax
        import jax.numpy as jnp
        _gk = jax.random.key(seed)
        x = -0.0003713 + 1 * jax.random.normal(jax.random.fold_in(_gk, 1), (3125, 256), jnp.float32)
        _s = jax.random.randint(jax.random.fold_in(_gk, 2), (50000,), 0, 3125, jnp.int32)
        _d = jax.random.randint(jax.random.fold_in(_gk, 3), (50000,), 0, 3125, jnp.int32)
        _loop = jnp.arange(3125, dtype=jnp.int32)
        src = jnp.concatenate([_s, _d, _loop])
        dst = jnp.concatenate([_d, _s, _loop])
        _o = jnp.argsort(dst, stable=True)
        src = src[_o]
        dst = dst[_o]
        edge_attr_18 = 0.00023367 + 0.999922 * jax.random.normal(jax.random.fold_in(_gk, 12), (103125, 18), jnp.float32)
        edge_attr_64 = 1.36993e-05 + 0.999972 * jax.random.normal(jax.random.fold_in(_gk, 13), (103125, 64), jnp.float32)
        edge_type_8 = jax.random.randint(jax.random.fold_in(_gk, 15), (103125,), 0, 8, jnp.int32)
        edge_weight = jax.random.uniform(jax.random.fold_in(_gk, 16), (103125,), jnp.float32, 0.0, 0.999998)
        return (x, src, dst, edge_attr_18, edge_attr_64, edge_type_8, edge_weight)
    x, src, dst, edge_attr_18, edge_attr_64, edge_type_8, edge_weight = _rec_inputs()

    def _L0_gnn_setup():
        import jax, jax.numpy as jnp
        import numpy as np
        N, E = (3125, 50000)
        DIM, H, D = (256, 16, 8)
        DH = D * H
        IN_RPE = 18
        SCALE = D ** (-0.5)
        EPS = 1e-16

        def _segment_softmax(compat, s, num_nodes):
            m = jax.ops.segment_max(compat, s, num_segments=num_nodes)
            ex = jnp.exp(compat - m[s])
            den = jax.ops.segment_sum(ex, s, num_segments=num_nodes)
            return ex / (den[s] + EPS)
        key = jax.random.key(seed)
        ks = jax.random.split(key, 10)
        x = jax.random.normal(ks[0], (N, DIM), dtype=jnp.float32)
        edge_index = jax.random.randint(ks[1], (2, E), 0, N, dtype=jnp.int64)
        edge_attr = jax.random.normal(ks[2], (E, IN_RPE), dtype=jnp.float32)
        Wqkv = jax.random.normal(ks[3], (DIM, 2 * DH + DIM), dtype=jnp.float32) * DIM ** (-0.5)
        bqkv = jnp.zeros((2 * DH + DIM,), dtype=jnp.float32)
        Wk_rpe = jax.random.normal(ks[4], (IN_RPE, DH), dtype=jnp.float32) * IN_RPE ** (-0.5)
        bk_rpe = jnp.zeros((DH,), dtype=jnp.float32)
        Wq_rpe = jax.random.normal(ks[5], (IN_RPE, DH), dtype=jnp.float32) * IN_RPE ** (-0.5)
        bq_rpe = jnp.zeros((DH,), dtype=jnp.float32)
        return {'x': x, 'edge_index': edge_index, 'edge_attr': edge_attr, 'Wqkv': Wqkv, 'bqkv': bqkv, 'Wk_rpe': Wk_rpe, 'bk_rpe': bk_rpe, 'Wq_rpe': Wq_rpe, 'bq_rpe': bq_rpe}
    _L0_gnn_all = _L0_gnn_setup()
    _L0_gnn_in = {k: v for k, v in _L0_gnn_all.items() if k in ('Wqkv', 'bqkv', 'Wk_rpe', 'bk_rpe', 'Wq_rpe', 'bq_rpe')}
    del _L0_gnn_all

    def _L1_gnn_setup():
        import jax, jax.numpy as jnp
        import numpy as np
        N = 1250
        E = 20000
        D = 256
        H = 8
        DH = D // H
        ED = 64
        FF = 4 * D
        EPS = 1e-05

        def _layernorm(x, g, b):
            m = jnp.mean(x, axis=-1, keepdims=True)
            v = jnp.var(x, axis=-1, keepdims=True)
            return (x - m) * jax.lax.rsqrt(v + EPS) * g + b

        def _edge_attention(xn, edge_index, ef, ew, Wq, bq, Wk, bk, Wv, bv, We, be, Wo, bo):
            n = xn.shape[0]
            scale = DH ** (-0.5)
            q = (xn @ Wq + bq).reshape(n, H, DH)
            k = (xn @ Wk + bk).reshape(n, H, DH)
            v = (xn @ Wv + bv).reshape(n, H, DH)
            src, dst = (edge_index[0], edge_index[1])
            ep = ef @ We + be
            scores = jnp.einsum('ehd,ehd->eh', q[dst], k[src] + ep[:, None, :]) * scale
            scores = scores * ew[:, None]
            m = jax.ops.segment_max(scores, dst, num_segments=n)
            m = jnp.where(jnp.isfinite(m), m, 0.0)
            ex = jnp.exp(scores - m[dst])
            s = jax.ops.segment_sum(ex, dst, num_segments=n)
            attn = ex / s[dst]
            out = jax.ops.segment_sum(attn[:, :, None] * v[src], dst, num_segments=n)
            out = out.reshape(n, D) @ Wo + bo
            return out
        key = jax.random.key(seed)
        ks = jax.random.split(key, 32)

        def lin_w(k, i, o):
            return (jax.random.normal(k, (i, o), jnp.float32) / np.sqrt(i)).astype(jnp.float32)
        return {'x': jax.random.normal(ks[0], (N, D), jnp.float32), 'edge_features': jax.random.normal(ks[1], (E, ED), jnp.float32), 'edge_weights': jax.random.uniform(ks[2], (E,), jnp.float32), 'edge_index': jax.random.randint(ks[3], (2, E), 0, N, dtype=jnp.int32), 'Wq': lin_w(ks[4], D, D), 'bq': jnp.zeros((D,), jnp.float32), 'Wk': lin_w(ks[5], D, D), 'bk': jnp.zeros((D,), jnp.float32), 'Wv': lin_w(ks[6], D, D), 'bv': jnp.zeros((D,), jnp.float32), 'We': lin_w(ks[7], ED, DH), 'be': jnp.zeros((DH,), jnp.float32), 'Wo': lin_w(ks[8], D, D), 'bo': jnp.zeros((D,), jnp.float32), 'ln1_g': jnp.ones((D,), jnp.float32), 'ln1_b': jnp.zeros((D,), jnp.float32), 'ln2_g': jnp.ones((D,), jnp.float32), 'ln2_b': jnp.zeros((D,), jnp.float32), 'W1': lin_w(ks[9], D, FF), 'b1': jnp.zeros((FF,), jnp.float32), 'W2': lin_w(ks[10], FF, D), 'b2': jnp.zeros((D,), jnp.float32), 'alpha': jnp.ones((1,), jnp.float32), 'beta': jnp.ones((1,), jnp.float32)}
    _L1_gnn_all = _L1_gnn_setup()
    _L1_gnn_in = {k: v for k, v in _L1_gnn_all.items() if k in ('Wq', 'bq', 'Wk', 'bk', 'Wv', 'bv', 'We', 'be', 'Wo', 'bo', 'ln1_g', 'ln1_b', 'ln2_g', 'ln2_b', 'W1', 'b1', 'W2', 'b2', 'alpha', 'beta')}
    del _L1_gnn_all

    def _L2_gnn_setup():
        import jax, jax.numpy as jnp
        import numpy as np
        N_NODES = 1250
        N_EDGES = 20000
        NUM_RELS = 8
        DIM = 256
        BN_EPS = 1e-05
        key = jax.random.key(seed)
        k1, k2, k3, k4, k5 = jax.random.split(key, 5)
        h = jax.random.normal(k1, (N_NODES, DIM), dtype=jnp.float32)
        weight = jax.random.normal(k2, (NUM_RELS, DIM, DIM), dtype=jnp.float32) * 0.05
        gamma = jnp.ones((DIM,), dtype=jnp.float32)
        beta = jnp.zeros((DIM,), dtype=jnp.float32)
        src = jax.random.randint(k3, (N_EDGES,), 0, N_NODES, dtype=jnp.int32)
        dst = jax.random.randint(k4, (N_EDGES,), 0, N_NODES, dtype=jnp.int32)
        rel = jax.random.randint(k5, (N_EDGES,), 0, NUM_RELS, dtype=jnp.int32)
        return {'h': h, 'weight': weight, 'gamma': gamma, 'beta': beta, 'src': src, 'dst': dst, 'rel': rel}
    _L2_gnn_all = _L2_gnn_setup()
    _L2_gnn_in = {k: v for k, v in _L2_gnn_all.items() if k in ('weight', 'gamma', 'beta')}
    del _L2_gnn_all

    def _L3_gnn_setup():
        import jax, jax.numpy as jnp
        import numpy as np
        N_NODES = 3125
        N_EDGES = 100000
        IN_FEATS = 256
        N_HEADS = 4
        OUT_FEATS = 64
        NEG_SLOPE = 0.2
        key = jax.random.key(seed)
        ks = jax.random.split(key, 8)
        x = jax.random.normal(ks[0], (N_NODES, IN_FEATS), dtype=jnp.float32)
        src = jax.random.randint(ks[1], (N_EDGES,), 0, N_NODES)
        dst = jax.random.randint(ks[2], (N_EDGES,), 0, N_NODES)
        scale = 1.0 / np.sqrt(IN_FEATS)
        W = jax.random.normal(ks[3], (IN_FEATS, N_HEADS * OUT_FEATS), dtype=jnp.float32) * scale
        attn_l = jax.random.normal(ks[4], (N_HEADS, OUT_FEATS), dtype=jnp.float32) * 0.1
        attn_r = jax.random.normal(ks[5], (N_HEADS, OUT_FEATS), dtype=jnp.float32) * 0.1
        bias = jnp.zeros((N_HEADS * OUT_FEATS,), dtype=jnp.float32)
        return {'x': x, 'src': src, 'dst': dst, 'W': W, 'attn_l': attn_l, 'attn_r': attn_r, 'bias': bias}
    _L3_gnn_all = _L3_gnn_setup()
    _L3_gnn_in = {k: v for k, v in _L3_gnn_all.items() if k in ('W', 'attn_l', 'attn_r', 'bias')}
    del _L3_gnn_all
    return {'x': x, 'src': src, 'dst': dst, 'edge_attr_18': edge_attr_18, 'edge_attr_64': edge_attr_64, 'edge_type_8': edge_type_8, 'edge_weight': edge_weight, 'L0_gnn_Wqkv': _L0_gnn_in['Wqkv'], 'L0_gnn_bqkv': _L0_gnn_in['bqkv'], 'L0_gnn_Wk_rpe': _L0_gnn_in['Wk_rpe'], 'L0_gnn_bk_rpe': _L0_gnn_in['bk_rpe'], 'L0_gnn_Wq_rpe': _L0_gnn_in['Wq_rpe'], 'L0_gnn_bq_rpe': _L0_gnn_in['bq_rpe'], 'L1_gnn_Wq': _L1_gnn_in['Wq'], 'L1_gnn_bq': _L1_gnn_in['bq'], 'L1_gnn_Wk': _L1_gnn_in['Wk'], 'L1_gnn_bk': _L1_gnn_in['bk'], 'L1_gnn_Wv': _L1_gnn_in['Wv'], 'L1_gnn_bv': _L1_gnn_in['bv'], 'L1_gnn_We': _L1_gnn_in['We'], 'L1_gnn_be': _L1_gnn_in['be'], 'L1_gnn_Wo': _L1_gnn_in['Wo'], 'L1_gnn_bo': _L1_gnn_in['bo'], 'L1_gnn_ln1_g': _L1_gnn_in['ln1_g'], 'L1_gnn_ln1_b': _L1_gnn_in['ln1_b'], 'L1_gnn_ln2_g': _L1_gnn_in['ln2_g'], 'L1_gnn_ln2_b': _L1_gnn_in['ln2_b'], 'L1_gnn_W1': _L1_gnn_in['W1'], 'L1_gnn_b1': _L1_gnn_in['b1'], 'L1_gnn_W2': _L1_gnn_in['W2'], 'L1_gnn_b2': _L1_gnn_in['b2'], 'L1_gnn_alpha': _L1_gnn_in['alpha'], 'L1_gnn_beta': _L1_gnn_in['beta'], 'L2_gnn_weight': _L2_gnn_in['weight'], 'L2_gnn_gamma': _L2_gnn_in['gamma'], 'L2_gnn_beta': _L2_gnn_in['beta'], 'L3_gnn_W': _L3_gnn_in['W'], 'L3_gnn_attn_l': _L3_gnn_in['attn_l'], 'L3_gnn_attn_r': _L3_gnn_in['attn_r'], 'L3_gnn_bias': _L3_gnn_in['bias']}

def reference(x, src, dst, edge_attr_18, edge_attr_64, edge_type_8, edge_weight, L0_gnn_Wqkv, L0_gnn_bqkv, L0_gnn_Wk_rpe, L0_gnn_bk_rpe, L0_gnn_Wq_rpe, L0_gnn_bq_rpe, L1_gnn_Wq, L1_gnn_bq, L1_gnn_Wk, L1_gnn_bk, L1_gnn_Wv, L1_gnn_bv, L1_gnn_We, L1_gnn_be, L1_gnn_Wo, L1_gnn_bo, L1_gnn_ln1_g, L1_gnn_ln1_b, L1_gnn_ln2_g, L1_gnn_ln2_b, L1_gnn_W1, L1_gnn_b1, L1_gnn_W2, L1_gnn_b2, L1_gnn_alpha, L1_gnn_beta, L2_gnn_weight, L2_gnn_gamma, L2_gnn_beta, L3_gnn_W, L3_gnn_attn_l, L3_gnn_attn_r, L3_gnn_bias):
    import jax
    import jax.numpy as jnp

    def _L0_gnn_ref(x, edge_index, edge_attr, Wqkv, bqkv, Wk_rpe, bk_rpe, Wq_rpe, bq_rpe):
        import jax, jax.numpy as jnp
        import numpy as np
        N, E = (3125, 50000)
        DIM, H, D = (256, 16, 8)
        DH = D * H
        IN_RPE = 18
        SCALE = D ** (-0.5)
        EPS = 1e-16

        def _segment_softmax(compat, s, num_nodes):
            m = jax.ops.segment_max(compat, s, num_segments=num_nodes)
            ex = jnp.exp(compat - m[s])
            den = jax.ops.segment_sum(ex, s, num_segments=num_nodes)
            return ex / (den[s] + EPS)
        n = x.shape[0]
        e = edge_index.shape[1]
        qkv = x @ Wqkv + bqkv
        q = qkv[:, :DH].reshape(n, H, D)
        k = qkv[:, DH:2 * DH].reshape(n, H, D)
        v = qkv[:, 2 * DH:].reshape(n, H, DIM // H)
        s, t = (edge_index[0], edge_index[1])
        qe = q[s] * SCALE
        ke = k[t]
        ke = ke + (edge_attr @ Wk_rpe + bk_rpe).reshape(e, H, D)
        qe = qe + (edge_attr @ Wq_rpe + bq_rpe).reshape(e, H, D)
        compat = jnp.einsum('ehd,ehd->eh', qe, ke)
        attn = _segment_softmax(compat, s, n)
        msg = (v[t] * attn[..., None]).reshape(e, DIM)
        out = jax.ops.segment_sum(msg, s, num_segments=n)
        return out

    def _L1_gnn_ref(x, edge_features, edge_weights, edge_index, Wq, bq, Wk, bk, Wv, bv, We, be, Wo, bo, ln1_g, ln1_b, ln2_g, ln2_b, W1, b1, W2, b2, alpha, beta):
        import jax, jax.numpy as jnp
        import numpy as np
        N = 1250
        E = 20000
        D = 256
        H = 8
        DH = D // H
        ED = 64
        FF = 4 * D
        EPS = 1e-05

        def _layernorm(x, g, b):
            m = jnp.mean(x, axis=-1, keepdims=True)
            v = jnp.var(x, axis=-1, keepdims=True)
            return (x - m) * jax.lax.rsqrt(v + EPS) * g + b

        def _edge_attention(xn, edge_index, ef, ew, Wq, bq, Wk, bk, Wv, bv, We, be, Wo, bo):
            n = xn.shape[0]
            scale = DH ** (-0.5)
            q = (xn @ Wq + bq).reshape(n, H, DH)
            k = (xn @ Wk + bk).reshape(n, H, DH)
            v = (xn @ Wv + bv).reshape(n, H, DH)
            src, dst = (edge_index[0], edge_index[1])
            ep = ef @ We + be
            scores = jnp.einsum('ehd,ehd->eh', q[dst], k[src] + ep[:, None, :]) * scale
            scores = scores * ew[:, None]
            m = jax.ops.segment_max(scores, dst, num_segments=n)
            m = jnp.where(jnp.isfinite(m), m, 0.0)
            ex = jnp.exp(scores - m[dst])
            s = jax.ops.segment_sum(ex, dst, num_segments=n)
            attn = ex / s[dst]
            out = jax.ops.segment_sum(attn[:, :, None] * v[src], dst, num_segments=n)
            out = out.reshape(n, D) @ Wo + bo
            return out
        xn = _layernorm(x, ln1_g, ln1_b)
        attn_out = _edge_attention(xn, edge_index, edge_features, edge_weights, Wq, bq, Wk, bk, Wv, bv, We, be, Wo, bo)
        x = x + alpha * attn_out
        xn = _layernorm(x, ln2_g, ln2_b)
        ff = jax.nn.gelu(xn @ W1 + b1, approximate=False) @ W2 + b2
        x = x + beta * ff
        return x

    def _L2_gnn_ref(h, weight, gamma, beta, src, dst, rel):
        import jax, jax.numpy as jnp
        import numpy as np
        N_NODES = 1250
        N_EDGES = 20000
        NUM_RELS = 8
        DIM = 256
        BN_EPS = 1e-05
        all_h = jnp.einsum('ni,rio->nro', h, weight)
        msg = all_h[src, rel]
        agg = jax.ops.segment_sum(msg, dst, num_segments=h.shape[0])
        mean = jnp.mean(agg, axis=0)
        var = jnp.mean(jnp.square(agg - mean), axis=0)
        out = (agg - mean) * jax.lax.rsqrt(var + BN_EPS) * gamma + beta
        return out

    def _L3_gnn_ref(x, src, dst, W, attn_l, attn_r, bias):
        import jax, jax.numpy as jnp
        import numpy as np
        N_NODES = 3125
        N_EDGES = 100000
        IN_FEATS = 256
        N_HEADS = 4
        OUT_FEATS = 64
        NEG_SLOPE = 0.2
        N = x.shape[0]
        H, D = attn_l.shape
        feat = (x @ W).reshape(N, H, D)
        el = (feat * attn_l[None]).sum(-1)
        er = (feat * attn_r[None]).sum(-1)
        e = jax.nn.leaky_relu(el[src] + er[dst], negative_slope=NEG_SLOPE)
        m = jax.ops.segment_max(e, dst, num_segments=N)
        m = jnp.where(jnp.isfinite(m), m, 0.0)
        ex = jnp.exp(e - m[dst])
        s = jax.ops.segment_sum(ex, dst, num_segments=N)
        alpha = ex / s[dst]
        msg = feat[src] * alpha[..., None]
        out = jax.ops.segment_sum(msg, dst, num_segments=N)
        out = out + bias.reshape(1, H, D)
        return out.reshape(N, H * D)
    edge_index = jnp.stack([src, dst])
    h = jnp.maximum(_layernorm(x, axis=-1), 0.0)
    x = x + _L0_gnn_ref(h, edge_index, edge_attr_18, L0_gnn_Wqkv, L0_gnn_bqkv, L0_gnn_Wk_rpe, L0_gnn_bk_rpe, L0_gnn_Wq_rpe, L0_gnn_bq_rpe)
    h = jnp.maximum(_layernorm(x, axis=-1), 0.0)
    x = x + _L1_gnn_ref(h, edge_attr_64, edge_weight, edge_index, L1_gnn_Wq, L1_gnn_bq, L1_gnn_Wk, L1_gnn_bk, L1_gnn_Wv, L1_gnn_bv, L1_gnn_We, L1_gnn_be, L1_gnn_Wo, L1_gnn_bo, L1_gnn_ln1_g, L1_gnn_ln1_b, L1_gnn_ln2_g, L1_gnn_ln2_b, L1_gnn_W1, L1_gnn_b1, L1_gnn_W2, L1_gnn_b2, L1_gnn_alpha, L1_gnn_beta)
    h = jnp.maximum(_layernorm(x, axis=-1), 0.0)
    x = x + _L2_gnn_ref(h, L2_gnn_weight, L2_gnn_gamma, L2_gnn_beta, src, dst, edge_type_8)
    h = jnp.maximum(_layernorm(x, axis=-1), 0.0)
    x = x + _L3_gnn_ref(h, src, dst, L3_gnn_W, L3_gnn_attn_l, L3_gnn_attn_r, L3_gnn_bias)
    return x

_drawn_inputs = setup_inputs


def setup_inputs(seed=0):
    import zlib

    import numpy as np

    out = dict(_drawn_inputs(seed))
    spreads = {'L0_gnn_bqkv': (0.0, 0.1),
     'L0_gnn_bk_rpe': (0.0, 0.1),
     'L0_gnn_bq_rpe': (0.0, 0.1),
     'L1_gnn_bq': (0.0, 0.499),
     'L1_gnn_bk': (0.0, 0.8),
     'L1_gnn_bv': (0.0, 0.1),
     'L1_gnn_be': (0.0, 0.8),
     'L1_gnn_bo': (0.0, 0.1),
     'L1_gnn_ln1_g': (1.0, 0.2),
     'L1_gnn_ln1_b': (0.0, 0.1),
     'L1_gnn_ln2_g': (1.0, 0.2),
     'L1_gnn_ln2_b': (0.0, 0.1),
     'L1_gnn_b1': (0.0, 0.1),
     'L1_gnn_b2': (0.0, 0.1),
     'L2_gnn_gamma': (1.0, 0.2),
     'L2_gnn_beta': (0.0, 0.1),
     'L3_gnn_bias': (0.0, 0.1)}
    factors = {'L3_gnn_attn_l': 3.137, 'L3_gnn_attn_r': 7.823}
    for name, (base, spread) in spreads.items():
        noise = np.random.default_rng([zlib.crc32(name.encode()), seed]).standard_normal(out[name].shape)
        drawn = base * np.exp(spread * noise) if base else spread * noise
        out[name] = jnp.asarray(drawn.astype(out[name].dtype))
    for name, factor in factors.items():
        out[name] = (out[name] * factor).astype(out[name].dtype)
    return out
```

```python
from contextlib import ExitStack, contextmanager

import concourse.bass as bass
from concourse import mybir

F32 = mybir.dt.float32
BF16 = mybir.dt.bfloat16
I32 = mybir.dt.int32
ALU = mybir.AluOpType
ACT = mybir.ActivationFunctionType
AX_X = mybir.AxisListType.X

P = 128
N, DIM, E = 3125, 256, 103125
NB = -(-N // P)
NR = NB * P
LAST = N - (NB - 1) * P
G = 8
T = 816
STEPS = T // G
BUFS = 3
EP = T * P
TB = -(-T // P)
TLAST = T - (TB - 1) * P
MAIN = 800
REST = E - MAIN * P
RCOL, RLAST = REST // P, REST % P
BIG = 1e30
DEN_EPS = 1e-16
LN_EPS = 1e-5
WP = DIM + 32

ONE, SEG, KEY, IDX, IDX_REL, WEIGHT = range(6)


class Order:

    def __init__(self, attrs, width):
        self.attrs, self.width = attrs, width


class Layer:
    def __init__(self, kind, heads, order, q_width, kv_width, koff):
        self.kind, self.heads, self.order = kind, heads, order
        self.q_width, self.kv_width, self.koff = q_width, kv_width, koff
        self.out_width = DIM + 2 * heads
        self.msg_width = DIM + heads


@contextmanager
def phase(nc, label):
    sems = []

    with ExitStack() as ctx:
        class Ph:
            @staticmethod
            def sbuf(name, shape, dt=F32):
                return ctx.enter_context(nc.sbuf_tensor(f"{label}_{name}", shape, dt))

            @staticmethod
            def sem(name):
                s = nc.alloc_semaphore(f"{label}_{name}")
                sems.append(s)
                return s

            @staticmethod
            def block():
                return nc.Block()
        yield Ph
        nc.clear_and_free_semaphores(sems)
        nc.all_engine_barrier()


def bc(ap, n):
    return ap.unsqueeze(len(ap.shape)).to_broadcast([*ap.shape, n])


def repeated(eng, count):
    yield 0
    with eng.Fori(1, count) as step:
        yield step


def build_constants(nc, C):
    with phase(nc, "const") as ph:
        pool_step = ph.sem("pool_step")
        with ph.block() as block:
            @block.gpsimd
            def _(pool):
                n = [0]

                def link(ins):
                    n[0] += 1
                    ins.then_inc(pool_step, 1)
                    pool.wait_ge(pool_step, n[0])

                for ident in (C.ident, C.ident_b):
                    link(pool.memset(ident[:], 0.0))
                    link(pool.affine_select(out=ident[:], in_=ident[:], compare_op=ALU.not_equal, fill=1.0,
                                            base=0, pattern=[[-1, P]], channel_multiplier=1))
                for tri, sign in ((C.lower, 1), (C.upper, -1)):
                    link(pool.memset(tri[:], 1.0))
                    link(pool.affine_select(out=tri[:], in_=tri[:], compare_op=ALU.is_gt, fill=0.0,
                                            base=0, pattern=[[-sign, P]], channel_multiplier=sign))
                link(pool.memset(C.ones[:], 1.0))
                link(pool.memset(C.zeros[:], 0.0))
                link(pool.memset(C.zeros_b[:], 0.0))
                link(pool.iota(C.iota_i[:], pattern=[[1, P]], base=0, channel_multiplier=0))
                link(pool.tensor_copy(C.iota[:], C.iota_i[:]))
                link(pool.tensor_copy(C.iota_b[:], C.iota[:]))


def sort_edges(nc, C, O, label, key_dram, other_dram, attr_dram, type_dram, weight_dram):
    A, W = O.attrs, O.width
    rel = type_dram is not None
    ps = C.psum
    with phase(nc, label) as ph:
        key_i = ph.sbuf("key_i", [P, T], I32)
        idx_i = ph.sbuf("idx_i", [P, T], I32)
        hi_i = ph.sbuf("hi_i", [P, T], I32)
        lo_i = ph.sbuf("lo_i", [P, T], I32)
        hi_b = ph.sbuf("hi_b", [P, T], BF16)
        lo_b = ph.sbuf("lo_b", [P, T], BF16)
        seg_f = ph.sbuf("seg_f", [P, T])
        if rel:
            type_i = ph.sbuf("type_i", [P, T], I32)
            rel_i = ph.sbuf("rel_i", [P, T], I32)
            weight = ph.sbuf("weight", [P, T])
        hot_hi = ph.sbuf("hot_hi", [P, 2, G, NB], BF16)
        hot_lo = ph.sbuf("hot_lo", [P, 2, G, P], BF16)
        hot_hi_t = ph.sbuf("hot_hi_t", [NB, 2, G, P])
        hist = ph.sbuf("hist", [NB, P])
        cum = ph.sbuf("cum", [NB, P])
        before_row = ph.sbuf("before_row", [NB, 1])
        starts = ph.sbuf("starts", [NB, P])
        table = ph.sbuf("table", [NB, 2, P])
        junk = ph.sbuf("junk", [P, 2, G, P], BF16)
        base = ph.sbuf("base", [P, 2, G])
        rank = ph.sbuf("rank", [P, 2, G])
        pos_i = ph.sbuf("pos_i", [P, 2, G], I32)
        rec = ph.sbuf("rec", [P, 2, G, W])
        reci = rec[:].bitcast(I32)
        seg_cur = ph.sbuf("seg_cur", [P, 2, G])
        seg_prev = ph.sbuf("seg_prev", [P, TB])
        seg_head = ph.sbuf("seg_head", [P, TB])

        filled = ph.sem("filled")
        loaded = ph.sem("loaded")
        dve_step = ph.sem("dve_step")
        split = ph.sem("split")
        hist_ready = ph.sem("hist_ready")
        hist_used = [ph.sem(f"hist_used{b}") for b in range(2)]
        sums = ph.sem("sums")
        starts_ready = ph.sem("starts_ready")
        with ph.block() as block:
            loads = [(key_i, key_dram), (idx_i, other_dram)]
            if rel:
                loads += [(type_i, type_dram), (weight, weight_dram)]

            @block.gpsimd
            def _(pool):
                pool.memset(key_i[:], N).then_inc(filled, 1)
                pool.memset(idx_i[:], N).then_inc(filled, 1)
                if rel:
                    pool.memset(type_i[:], 0).then_inc(filled, 1)
                    pool.memset(weight[:], 0.0).then_inc(filled, 1)
                pool.memset(rec[:], 0.0).then_inc(filled, 1)
                pool.memset(seg_prev[:], 0.0).then_inc(filled, 1)
                pool.memset(seg_head[:], 0.0).then_inc(filled, 1)

            @block.sync
            def _(sp):
                sp.wait_ge(filled, len(loads) + 3)
                for tile, dram in loads:
                    sp.dma_start(tile[:, 0:MAIN], dram[0:MAIN * P].rearrange("(p j) -> p j", j=MAIN)).then_inc(loaded, 16)
                    rest = dram[MAIN * P:MAIN * P + RCOL * P].rearrange("(g p o) -> g p o", p=P, o=1)
                    for g in range(RCOL):
                        sp.dma_start(tile[:, MAIN + g:MAIN + g + 1], rest[g]).then_inc(loaded, 16)
                    sp.dma_start(tile[0:RLAST, MAIN + RCOL:MAIN + RCOL + 1],
                                 dram[E - RLAST:E].rearrange("(p o) -> p o", o=1)).then_inc(loaded, 16)

            @block.vector
            def _(dve):
                n = [0]

                def link(ins):
                    n[0] += 1
                    ins.then_inc(dve_step, 1)
                    dve.wait_ge(dve_step, n[0])

                dve.wait_ge(loaded, 16 * len(loads) * (RCOL + 2))
                link(dve.tensor_scalar(hi_i[:], key_i[:], 7, None, ALU.arith_shift_right))
                link(dve.tensor_scalar(lo_i[:], key_i[:], P - 1, None, ALU.bitwise_and))
                link(dve.tensor_copy(hi_b[:], hi_i[:]))
                link(dve.tensor_copy(lo_b[:], lo_i[:]))
                link(dve.tensor_scalar(seg_f[:], key_i[:], 1.0, None, ALU.add))
                if rel:
                    link(dve.scalar_tensor_tensor(out=rel_i[:], in0=idx_i[:], scalar=8.0, in1=type_i[:],
                                                  op0=ALU.mult, op1=ALU.add))
                dve.memset(rec[:, :, :, A + ONE:A + ONE + 1], 1.0)

        with ph.block() as block:
            @block.vector
            def _(dve):
                for j in repeated(dve, STEPS // 2):
                    for b in range(2):
                        dve.wait_ge(hist_used[b], j)
                        cols = bass.ds(j * (2 * G) + b * G, G)
                        dve.tensor_tensor(hot_hi[:, b], C.iota_b[:, 0:NB].unsqueeze(1).to_broadcast([P, G, NB]),
                                          bc(hi_b[:, cols], NB), ALU.is_equal).then_inc(hist_ready, 1)
                        dve.tensor_tensor(hot_lo[:, b], C.iota_b[:].unsqueeze(1).to_broadcast([P, G, P]),
                                          bc(lo_b[:, cols], P), ALU.is_equal).then_inc(hist_ready, 1)

                dve.wait_ge(sums, 1)
                dve.tensor_copy(hist[:], ps[0:NB, 0, 0:P]).then_inc(dve_step, 1)
                done = 6 + rel
                dve.wait_ge(dve_step, done)
                dve.tensor_tensor_scan(cum[:], C.ones[0:NB, :], hist[:], 0.0, ALU.mult, ALU.add).then_inc(starts_ready, 1)
                dve.wait_ge(sums, 2)
                dve.tensor_copy(before_row[:], ps[0:NB, 1, 0:1]).then_inc(dve_step, 1)
                dve.wait_ge(dve_step, done + 1)
                dve.scalar_tensor_tensor(out=starts[:], in0=cum[:], scalar=before_row[:], in1=hist[:],
                                         op0=ALU.add, op1=ALU.subtract).then_inc(starts_ready, 1)
                dve.wait_ge(sums, 3)
                dve.tensor_scalar(O.home_i[:], ps[:, 2, 0:NB], float(EP - 1), None, ALU.min)
                dve.tensor_scalar(O.has_edges[:], ps[:, 2, P:P + NB], 0.0, None, ALU.is_gt)

            @block.tensor
            def _(pe):
                pe.matmul(ps[0:NB, 0, 0:P], C.zeros_b[:, 0:NB], C.zeros_b[:], start=True, stop=False,
                          skip_group_check=True)
                for j in repeated(pe, STEPS // 2):
                    for b in range(2):
                        pe.wait_ge(hist_ready, j * 4 + 2 * b + 2)
                        for c in range(G):
                            last = pe.matmul(ps[0:NB, 0, 0:P], hot_hi[:, b, c, :], hot_lo[:, b, c, :],
                                             start=False, stop=False, skip_group_check=True)
                        last.then_inc(hist_used[b], 1)
                pe.matmul(ps[0:NB, 0, 0:P], C.zeros_b[:, 0:NB], C.zeros_b[:], start=False, stop=True,
                          skip_group_check=True).then_inc(sums, 1)
                pe.wait_ge(starts_ready, 1)
                pe.matmul(ps[0:NB, 1, 0:1], C.upper[0:NB, 0:NB], cum[:, P - 1:P], start=True, stop=True).then_inc(sums, 1)
                pe.wait_ge(starts_ready, 2)
                pe.transpose(ps[:, 2, 0:NB], starts[:], C.ident[0:NB, 0:NB])
                pe.transpose(ps[:, 2, P:P + NB], hist[:], C.ident[0:NB, 0:NB]).then_inc(sums, 1)

        hot_ready = ph.sem("hot_ready")
        seg_ready = ph.sem("seg_ready")
        words_ready = ph.sem("words_ready")
        attrs_in = [ph.sem(f"attrs_in{b}") for b in range(2)]
        turned = ph.sem("turned")
        turned_copied = ph.sem("turned_copied")
        keys_ready = ph.sem("keys_ready")
        ranked = ph.sem("ranked")
        table_ready = ph.sem("table_ready")
        looked_up = ph.sem("looked_up")
        row_used = [ph.sem(f"row_used{b}") for b in range(2)]
        table_moved = ph.sem("table_moved")
        pos_ready = ph.sem("pos_ready")
        scattered = [ph.sem(f"scattered{b}") for b in range(2)]
        scatters_begun = ph.sem("scatters_begun")
        words_begun = ph.sem("words_begun")
        with ph.block() as block:
            attr_main = attr_dram[0:MAIN * P, :].rearrange("(p j) a -> p j a", j=MAIN)

            def at(j, b):
                return lambda k, o: j * (2 * k) + (b * k + o)

            def steps(eng, body):
                for j in repeated(eng, MAIN // G // 2):
                    body(j, 0, (j, 1), False)
                    body(j, 1, (j + 1, 0), False)
                j = MAIN // G // 2
                body(j, 0, (j, 1), True)
                body(j, 1, None, True)

            @block.sync
            def _(sp):
                def body(j, b, ahead, tail):
                    sp.wait_ge(scattered[b], j * P)
                    if not tail:
                        sp.dma_start(rec[:, b, :, 0:A], attr_main[:, bass.ds(j * (2 * G) + b * G, G), :]).then_inc(attrs_in[b], 16)
                    elif b == 0:
                        sp.dma_start(rec[:, b, 0:RCOL, 0:A],
                                     attr_dram[MAIN * P:MAIN * P + RCOL * P, :].rearrange("(g p) a -> p g a", p=P)).then_inc(attrs_in[b], 16)
                        sp.dma_start(rec[0:RLAST, b, RCOL, 0:A], attr_dram[E - RLAST:E, :]).then_inc(attrs_in[b], 16)
                steps(sp, body)

            @block.gpsimd
            def _(pool):
                def body(j, b, ahead, tail):
                    pool.wait_ge(words_ready, j * 2 + b + 1)
                    pool.wait_ge(attrs_in[b], (j + (2 if tail and b == 0 else 0 if tail else 1)) * 16)
                    pool.wait_ge(pos_ready, j * 2 + b + 1)
                    pool.sem_inc(scatters_begun, 1)
                    for c in range(G):
                        pool.indirect_dma_start(O.rec, bass.IndirectOffsetOnAxis(ap=pos_i[:, b, c:c + 1], axis=0),
                                                rec[:, b, c, :], None).then_inc(scattered[b], 16)
                steps(pool, body)
                for b in range(2):
                    pool.wait_ge(scattered[b], (STEPS // 2) * P)

            @block.scalar
            def _(act):
                act.copy(table[:, 0, :], starts[:]).then_inc(table_ready, 1)

                def keys(j, b):
                    act.copy(seg_cur[:, b, :], seg_f[:, bass.ds(j * (2 * G) + b * G, G)]).then_inc(seg_ready, 1)

                def turn(j, b, h):
                    act.wait_ge(turned, at(j, b)(2, h + 1))
                    act.copy(hot_hi_t[:, b, 4 * h:4 * h + 4, :], ps[0:NB, h, :].rearrange("k (c e) -> k c e", c=4)).then_inc(turned_copied, 1)

                keys(0, 0)
                turn(0, 0, 0)
                turn(0, 0, 1)

                def body(j, b, ahead, tail):
                    n = at(j, b)
                    cols = bass.ds(j * (2 * G) + b * G, G)
                    for c in range(G):
                        act.wait_ge(table_moved, n(G, c + 1))
                        act.copy(table[:, (c + 1) % 2, :], ps[0:NB, 6, 0:P]).then_inc(table_ready, 1)
                        if ahead and c == 2:
                            if not (isinstance(j, int) and j == 0 and b == 0):
                                act.wait_ge(pos_ready, n(1, 0))
                            keys(*ahead)
                        if ahead and c in (5, 6):
                            turn(*ahead, c - 5)
                    words = [(SEG, seg_f, rec), (KEY, key_i, reci), (IDX, idx_i, reci)]
                    if rel:
                        words += [(IDX_REL, rel_i, reci), (WEIGHT, weight, rec)]
                    act.wait_ge(scattered[b], j * P)
                    act.sem_inc(words_begun, 1)
                    for w, src, dst in words:
                        last = act.copy(dst[:, b, :, A + w], src[:, cols])
                    last.then_inc(words_ready, 1)
                steps(act, body)

            @block.vector
            def _(dve):
                def one_hots(j, b):
                    cols = bass.ds(j * (2 * G) + b * G, G)
                    dve.tensor_tensor(hot_hi[:, b], C.iota_b[:, 0:NB].unsqueeze(1).to_broadcast([P, G, NB]),
                                      bc(hi_b[:, cols], NB), ALU.is_equal).then_inc(hot_ready, 1)
                    dve.tensor_tensor(hot_lo[:, b], C.iota_b[:].unsqueeze(1).to_broadcast([P, G, P]),
                                      bc(lo_b[:, cols], P), ALU.is_equal).then_inc(hot_ready, 1)

                one_hots(0, 0)

                def body(j, b, ahead, tail):
                    n = at(j, b)
                    for h in range(2):
                        dve.wait_ge(keys_ready, n(2, h + 1))
                        for c in range(4 * h, 4 * h + 4):
                            last = dve.scalar_tensor_tensor(out=junk[:, 0, c], in0=ps[:, 4 + h, P * (c % 4):P * (c % 4) + P],
                                                            scalar=seg_cur[:, b, c:c + 1], in1=C.lower[:],
                                                            op0=ALU.is_equal, op1=ALU.mult, accum_out=rank[:, b, c:c + 1])
                        last.then_inc(ranked, 1)
                        for c in range(4 * h, 4 * h + 4):
                            dve.wait_ge(looked_up, n(G, c + 1))
                            dve.scalar_tensor_tensor(out=junk[:, 1, c], in0=ps[:, 2 + c % 2, 0:P], scalar=1.0,
                                                     in1=hot_lo[:, b, c, :], op0=ALU.mult, op1=ALU.mult,
                                                     accum_out=base[:, b, c:c + 1]).then_inc(row_used[c % 2], 1)
                            if c == 1 and ahead:
                                one_hots(*ahead)
                    dve.wait_ge(ranked, n(2, 2))
                    for h in range(2):
                        dve.wait_ge(row_used[h], n(4, 4))
                    dve.wait_ge(scattered[b], j * P)
                    dve.tensor_tensor(pos_i[:, b, :], base[:, b, :], rank[:, b, :], ALU.add).then_inc(pos_ready, 1)
                steps(dve, body)

            @block.tensor
            def _(pe):
                pe.matmul(ps[0:NB, 6, 0:P], C.ident[0:NB, 0:NB], starts[:], start=True, stop=False, skip_group_check=True)

                def turn(j, b, h):
                    pe.wait_ge(hot_ready, at(j, b)(2, 2))
                    for c in range(4):
                        last = pe.matmul(ps[0:NB, h, P * c:P * c + P], hot_hi[:, b, 4 * h + c, :], C.ident_b[:],
                                         start=True, stop=True)
                    last.then_inc(turned, 1)

                def keys(j, b, h, first=False):
                    pe.wait_ge(seg_ready, at(j, b)(1, 1))
                    if not first:
                        pe.wait_ge(ranked, at(j, b)(2, h) - 1)
                    for c in range(4):
                        last = pe.matmul(ps[:, 4 + h, P * c:P * c + P], seg_cur[:, b, 4 * h + c:4 * h + c + 1].to_broadcast([P, P]),
                                         C.ident[:], start=True, stop=True)
                    last.then_inc(keys_ready, 1)

                turn(0, 0, 0)
                turn(0, 0, 1)
                keys(0, 0, 0, True)
                keys(0, 0, 1, True)

                def body(j, b, ahead, tail):
                    n = at(j, b)
                    pe.wait_ge(turned_copied, n(2, 2))
                    for c in range(G):
                        pe.wait_ge(table_ready, n(G, c + 1))
                        pe.matmul(ps[0:NB, 6, 0:P], hot_hi[:, b, c, :], hot_lo[:, b, c, :],
                                  start=False, stop=False, skip_group_check=True).then_inc(table_moved, 1)
                        pe.wait_ge(row_used[c % 2], n(4, c // 2))
                        pe.matmul(ps[:, 2 + c % 2, 0:P], hot_hi_t[:, b, c, :], table[:, c % 2, :],
                                  start=True, stop=True).then_inc(looked_up, 1)
                        if ahead and c in (3, 4):
                            turn(*ahead, c - 3)
                        if ahead and c in (5, 6):
                            keys(*ahead, c - 5)
                steps(pe, body)

        head_in = ph.sem("head_in")
        cont_step = ph.sem("cont_step")
        cont_rows = ph.sem("cont_rows")
        with ph.block() as block:
            seg_word = O.rec.rearrange("(t q) w -> q t w", q=P)[:, :, A + SEG]

            @block.sync
            def _(sp):
                with nc.allow_non_contiguous_dma(reason="one word per tile"):
                    for t0, tile, q, lag in ((0, seg_head, 0, 0), (0, seg_prev, P - 1, 1)):
                        for k in range(TB):
                            first, last = max(k * P - lag, 0), min((k + 1) * P, T) - lag
                            p0 = lag if k == 0 else 0
                            sp.dma_start(tile[p0:p0 + last - first, k:k + 1],
                                         seg_word[q, first:last].rearrange("(t o) -> t o", o=1)).then_inc(head_in, 16)

            @block.vector
            def _(dve):
                dve.wait_ge(head_in, 16 * 2 * TB)
                dve.tensor_tensor(seg_prev[:], seg_prev[:], seg_head[:], ALU.is_equal).then_inc(cont_step, 1)
                dve.wait_ge(cont_step, 1)
                dve.tensor_tensor(O.cont_key[:], seg_prev[:], seg_head[:], ALU.mult).then_inc(cont_step, 1)
                dve.wait_ge(cont_rows, 1)
                dve.tensor_copy(O.cont_row[:, 0:512], ps[0:16, 0, :]).then_inc(cont_step, 1)
                dve.tensor_copy(O.cont_row[:, 512:TB * P], ps[0:16, 1, 0:TB * P - 512]).then_inc(cont_step, 1)
                dve.memset(O.cont_pen[:], -BIG).then_inc(cont_step, 1)
                dve.wait_ge(cont_step, 5)
                dve.tensor_tensor(O.cont_pen[:, 1:TB * P], O.cont_row[:, 1:TB * P], O.cont_row[:, 0:TB * P - 1],
                                  ALU.not_equal).then_inc(cont_step, 1)
                dve.wait_ge(cont_step, 6)
                dve.tensor_scalar(O.cont_pen[:, 1:TB * P], O.cont_pen[:, 1:TB * P], -BIG, None, ALU.mult)

            @block.tensor
            def _(pe):
                pe.wait_ge(cont_step, 2)
                for k in range(TB):
                    last = pe.matmul(ps[0:16, k // 4, P * (k % 4):P * (k % 4) + P],
                                     O.cont_key[:, k:k + 1].to_broadcast([P, 16]), C.ident[:], start=True, stop=True)
                last.then_inc(cont_rows, 1)


class Consts:
    pass


def make_constants(nc, ctx):
    def sb(name, shape, dt=F32):
        return ctx.enter_context(nc.sbuf_tensor(name, shape, dt))

    C = Consts()
    C.psum = ctx.enter_context(nc.psum_tensor("banks", [P, 8, 512], F32))
    C.ident, C.ident_b = sb("ident", [P, P]), sb("ident_b", [P, P], BF16)
    C.lower, C.upper = sb("lower", [P, P]), sb("upper", [P, P])
    C.ones, C.zeros = sb("ones", [P, P]), sb("zeros", [P, P])
    C.zeros_b = sb("zeros_b", [P, P], BF16)
    C.iota, C.iota_i, C.iota_b = sb("iota", [P, P]), sb("iota_i", [P, P], I32), sb("iota_b", [P, P], BF16)
    return C


def make_order(nc, ctx, label, attrs, width):
    def sb(name, shape, dt=F32):
        return ctx.enter_context(nc.sbuf_tensor(f"{label}_{name}", shape, dt))

    O = Order(attrs, width)
    O.rec = nc.dram_tensor(f"{label}_records", (EP, width), F32, kind="Internal").ap()
    O.home_i, O.has_edges = sb("home", [P, NB], I32), sb("has_edges", [P, NB])
    O.cont_key, O.cont_row, O.cont_pen = sb("cont_key", [P, TB]), sb("cont_row", [16, TB * P]), sb("cont_pen", [16, TB * P + 1])
    return O


def edge_layer(nc, C, L, label, tabs, weights):
    kind, H, O, koff = L.kind, L.heads, L.order, L.koff
    W, MW, ps = O.width, L.msg_width, C.psum
    attr_layer = kind in (0, 1)
    word0 = 0 if attr_layer else O.attrs
    RW = W - word0
    seg, key, idx = (O.attrs - word0 + w for w in (SEG, KEY, IDX_REL if kind == 2 else IDX))
    K = O.attrs + 1
    KW = {0: DIM, 1: DIM // L.heads if H else 0}.get(kind, 0)
    HG = G * H
    dh = DIM // H if H else 0
    gathers = 1 if kind == 2 else 2
    with phase(nc, label) as ph:
        rec = ph.sbuf("rec", [P, BUFS, G, RW])
        reci = rec[:].bitcast(I32)
        kv = ph.sbuf("kv", [P, BUFS, G, koff + MW])
        q = ph.sbuf("q", [P, BUFS, G, L.q_width]) if L.q_width else None
        same = ph.sbuf("same", [P, BUFS, G, P])
        outs = ph.sbuf("outs", [P, BUFS, G, L.out_width])
        if attr_layer:
            w_attr = ph.sbuf("w_attr", [K, KW])
            attr_t = ph.sbuf("attr_t", [K, G, P])
            attr_sum = ph.sbuf("attr_sum", [P, G, KW])
            prod = ph.sbuf("prod", [P, G, L.q_width])
        if H:
            score = ph.sbuf("score", [P, G, H])
            seg_wide = ph.sbuf("seg_wide", [P, G, H])
            score_raw = ph.sbuf("score_raw", [P, G, H])
            seg_t = ph.sbuf("seg_t", [HG, P])
            pen = ph.sbuf("pen", [HG, P + 1])
            run_max = ph.sbuf("run_max", [HG, P])
            seg_max = ph.sbuf("seg_max", [HG, P])
            below = ph.sbuf("below", [HG, P])
            expo = ph.sbuf("expo", [HG, P])

        weights_in = ph.sem("weights_in")
        pen_set = ph.sem("pen_set")
        rec_in = [ph.sem(f"rec_in{b}") for b in range(BUFS)]
        gathered = [[ph.sem(f"gathered{b}{h}") for h in range(2)] for b in range(BUFS)]
        gathers_begun = ph.sem("gathers_begun")
        same_keys = ph.sem("same_keys")
        same_done = [ph.sem(f"same_done{h}") for h in range(2)]
        msg_done = ph.sem("msg_done")
        summed = [ph.sem(f"summed{b}") for b in range(BUFS)]
        out_free = [ph.sem(f"out_free{b}") for b in range(2)]
        out_copied = ph.sem("out_copied")
        stored = [ph.sem(f"stored{b}") for b in range(BUFS)]
        dve_step = ph.sem("dve_step")
        act_step = ph.sem("act_step")
        if attr_layer:
            attr_turned = ph.sem("attr_turned")
            attr_copied = ph.sem("attr_copied")
            attr_mult = ph.sem("attr_mult")
            attr_moved = ph.sem("attr_moved")
            attr_begun = ph.sem("attr_begun")
        if H:
            seg_wide_done = ph.sem("seg_wide_done")
            seg_turned = ph.sem("seg_turned")
            seg_copied = ph.sem("seg_copied")
            pen_done = ph.sem("pen_done")
            score_done = ph.sem("score_done")
            score_turned = ph.sem("score_turned")
            below_done = ph.sem("below_done")
            exp_done = ph.sem("exp_done")
            exp_turned = ph.sem("exp_turned")
            turns_begun = ph.sem("turns_begun")
            max_copied = ph.sem("max_copied")

        MULTS = {0: 4, 1: 1}.get(kind, 0)

        def at(j, b):
            return lambda k, o: j * (BUFS * k) + (b * k + o)

        ROUNDS = STEPS // BUFS

        def steps(eng, body):
            for j in repeated(eng, ROUNDS - 1):
                for b in range(BUFS):
                    body(j, b, (j, b + 1) if b < BUFS - 1 else (j + 1, 0))
            for b in range(BUFS):
                body(ROUNDS - 1, b, (ROUNDS - 1, b + 1) if b < BUFS - 1 else None)

        with ph.block() as block:
            @block.sync
            def _(sp):
                if attr_layer:
                    col = 0
                    for w, bias in weights:
                        n_cols = w.shape[1]
                        sp.dma_start(w_attr[0:K - 1, col:col + n_cols], w).then_inc(weights_in, 16)
                        sp.dma_start(w_attr[K - 1:K, col:col + n_cols], bias.rearrange("(o n) -> o n", o=1)).then_inc(weights_in, 16)
                        col += n_cols
                records = O.rec.rearrange("(t p) w -> p t w", p=P)

                def body(j, b, ahead):
                    sp.wait_ge(summed[b], j * G)
                    sp.dma_start(rec[:, b], records[:, bass.ds(j * (BUFS * G) + b * G, G), word0:W]).then_inc(rec_in[b], 16)
                steps(sp, body)

            @block.gpsimd
            def _(pool):
                def body(j, b, ahead):
                    pool.wait_ge(rec_in[b], j * 16 + 16)
                    pool.sem_inc(gathers_begun, 1)
                    for c in range(G):
                        pool.indirect_dma_start(kv[:, b, c, 0:L.kv_width], None, tabs[0],
                                                bass.IndirectOffsetOnAxis(ap=reci[:, b, c, idx:idx + 1], axis=0)
                                                ).then_inc(gathered[b][c // 4], 16)
                        if gathers == 2:
                            pool.indirect_dma_start(q[:, b, c, :], None, tabs[1],
                                                    bass.IndirectOffsetOnAxis(ap=reci[:, b, c, key:key + 1], axis=0)
                                                    ).then_inc(gathered[b][c // 4], 16)
                steps(pool, body)

            @block.tensor
            def _(pe):
                if attr_layer:
                    pe.wait_ge(weights_in, 32 * len(weights))

                def front(j, b):
                    n = at(j, b)
                    pe.wait_ge(rec_in[b], j * 16 + 16)
                    for h in range(2):
                        pe.wait_ge(same_done[h], n(1, 0))
                        for c in range(4):
                            last = pe.matmul(ps[:, 3 + 2 * h, P * c:P * c + P],
                                             rec[:, b, 4 * h + c, seg:seg + 1].to_broadcast([P, P]), C.ident[:],
                                             start=True, stop=True)
                        last.then_inc(same_keys, 1)
                    if H:
                        if attr_layer:
                            pe.wait_ge(attr_copied, n(2, 0))
                        else:
                            pe.wait_ge(seg_copied, n(1, 0))
                        pe.wait_ge(seg_wide_done, n(1, 1))
                        pe.matmul(ps[0:HG, 0, 0:P], seg_wide[:].rearrange("p g h -> p (g h)"), C.ident[:],
                                  start=True, stop=True).then_inc(seg_turned, 1)
                    for h in range(2 if attr_layer else 0):
                        if h == 0:
                            pe.wait_ge(seg_copied, n(1, 1))
                        else:
                            pe.wait_ge(attr_copied, n(2, 1))
                        for c in range(4):
                            last = pe.transpose(ps[0:K, 0, P * c:P * c + P], rec[:, b, 4 * h + c, 0:K], C.ident[:])
                        last.then_inc(attr_turned, 1)

                def products(j, b, m, first=False):
                    n = at(j, b)
                    if kind == 0:
                        pe.wait_ge(attr_copied, n(2, m // 2 + 1))
                        if m > 1 or not first:
                            pe.wait_ge(attr_moved, n(4, m) - 1)
                        for c in range(2):
                            last = pe.matmul(ps[:, 1 + m % 2, KW * c:KW * c + KW], attr_t[:, 2 * m + c, :],
                                             w_attr[:], start=True, stop=True)
                        last.then_inc(attr_mult, 1)
                    elif kind == 1 and m == 0:
                        pe.wait_ge(attr_copied, n(2, 2))
                        pe.wait_ge(attr_moved, n(1, 0))
                        for c in range(G):
                            last = pe.matmul(ps[:, 1, KW * c:KW * c + KW], attr_t[:, c, :], w_attr[:], start=True, stop=True)
                        last.then_inc(attr_mult, 1)

                front(0, 0)
                for m in range(MULTS):
                    products(0, 0, m, True)

                def body(j, b, ahead):
                    n = at(j, b)
                    if ahead:
                        front(*ahead)
                    if H:
                        pe.wait_ge(max_copied, n(1, 0))
                        pe.wait_ge(score_done, n(1, 1))
                        pe.sem_inc(turns_begun, 1)
                        pe.transpose(ps[0:HG, 4, P:2 * P], score[:].rearrange("p g h -> p (g h)"), C.ident[:]).then_inc(score_turned, 1)
                        if ahead and MULTS:
                            products(*ahead, 0)
                        pe.wait_ge(exp_done, n(1, 1))
                        pe.sem_inc(turns_begun, 1)
                        pe.transpose(ps[:, 4, 2 * P:2 * P + HG], expo[:], C.ident[0:HG, 0:HG])
                        pe.transpose(ps[:, 4, 3 * P:3 * P + HG], seg_max[:], C.ident[0:HG, 0:HG]).then_inc(exp_turned, 1)
                        for m in range(1, MULTS if ahead else 0):
                            products(*ahead, m)
                    for c in range(G):
                        if c % 4 == 0:
                            if H:
                                pe.wait_ge(msg_done, n(2, c // 4 + 1))
                            else:
                                pe.wait_ge(gathered[b][c // 4], j * (64 * gathers) + 64 * gathers)
                                pe.wait_ge(same_done[c // 4], n(1, 1))
                        pe.wait_ge(out_free[c % 2], n(4, c // 2))
                        pe.matmul(ps[:, 6 + c % 2, 0:MW], same[:, b, c, :], kv[:, b, c, koff:koff + MW],
                                  start=True, stop=True).then_inc(summed[b], 1)
                steps(pe, body)

            @block.vector
            def _(dve):
                if H:
                    dve.memset(pen[:], -BIG).then_inc(pen_set, 1)
                    dve.wait_ge(pen_set, 1)
                links = {0: 4, 1: 5, 3: 3}.get(kind, 0)

                def wide(j, b):
                    dve.wait_ge(rec_in[b], j * 16 + 16)
                    dve.tensor_copy(seg_wide[:], rec[:, b, :, seg:seg + 1].to_broadcast([P, G, H])).then_inc(seg_wide_done, 1)

                def make_same(j, b, h):
                    dve.wait_ge(summed[b], j * G)
                    dve.wait_ge(same_keys, at(j, b)(2, h + 1))
                    dve.tensor_tensor(same[:, b, 4 * h:4 * h + 4, :], ps[:, 3 + 2 * h, :].rearrange("p (c e) -> p c e", c=4),
                                      rec[:, b, 4 * h:4 * h + 4, seg:seg + 1].to_broadcast([P, 4, P]),
                                      ALU.is_equal).then_inc(same_done[h], 1)

                def penalties(j, b):
                    dve.wait_ge(seg_copied, at(j, b)(1, 1))
                    dve.tensor_tensor(pen[:, 1:P], seg_t[:, 0:P - 1], seg_t[:, 1:P], ALU.subtract).then_inc(pen_done, 1)

                if H:
                    wide(0, 0)
                make_same(0, 0, 0)
                make_same(0, 0, 1)
                if H:
                    penalties(0, 0)

                def body(j, b, ahead):
                    n = at(j, b)
                    made = [0]

                    def link(ins):
                        made[0] += 1
                        ins.then_inc(dve_step, 1)
                        dve.wait_ge(dve_step, n(links, made[0]))

                    if not H:
                        if ahead:
                            make_same(*ahead, 0)
                            make_same(*ahead, 1)
                        return
                    if ahead:
                        wide(*ahead)
                    for h in range(2):
                        t = slice(4 * h, 4 * h + 4)
                        dve.wait_ge(gathered[b][h], j * 128 + 128)
                        if kind == 0:
                            dve.wait_ge(attr_moved, n(4, 2 * h + 2))
                            dve.tensor_tensor(kv[:, b, t, 0:P], attr_sum[:, t, 0:P], kv[:, b, t, 0:P], ALU.add)
                            last = dve.tensor_tensor(q[:, b, t, :], attr_sum[:, t, P:2 * P], q[:, b, t, :], ALU.add)
                        if kind == 1:
                            dve.wait_ge(attr_moved, n(1, 1))
                            k4 = kv[:, b, t, 0:DIM].rearrange("p c (h d) -> p c h d", h=H)
                            last = dve.tensor_tensor(k4, attr_sum[:, t, :].unsqueeze(2).to_broadcast([P, 4, H, KW]), k4, ALU.add)
                    if attr_layer:
                        link(last)
                        link(dve.tensor_tensor(prod[:], kv[:, b, :, 0:L.q_width], q[:, b], ALU.mult))
                        to = score_raw if kind == 1 else score
                        ins = dve.tensor_reduce(to[:], prod[:].rearrange("p g (h d) -> p g h d", h=H), AX_X, ALU.add)
                        if kind == 0:
                            ins.then_inc(score_done, 1)
                        else:
                            link(ins)
                            wt = rec[:, b, :, O.attrs + WEIGHT:O.attrs + WEIGHT + 1].to_broadcast([P, G, H])
                            dve.tensor_tensor(score[:], score_raw[:], wt, ALU.mult).then_inc(score_done, 1)
                    if kind == 3:
                        link(dve.tensor_tensor(score_raw[:], kv[:, b, :, 0:H], q[:, b], ALU.add))
                        dve.scalar_tensor_tensor(out=score[:], in0=score_raw[:], scalar=0.2, in1=score_raw[:],
                                                 op0=ALU.mult, op1=ALU.max).then_inc(score_done, 1)
                    if ahead:
                        make_same(*ahead, 0)
                    dve.wait_ge(score_turned, n(1, 1))
                    dve.wait_ge(pen_done, n(1, 1))
                    sc_t = ps[0:HG, 4, P:2 * P]
                    link(dve.tensor_tensor_scan(run_max[:], pen[:, 0:P], sc_t, -BIG, ALU.add, ALU.max))
                    link(dve.tensor_tensor_scan(seg_max[:, ::-1], pen[:, 1:P + 1][:, ::-1], run_max[:, ::-1], -BIG,
                                                ALU.add, ALU.max))
                    dve.tensor_tensor(below[:], sc_t, seg_max[:], ALU.subtract).then_inc(below_done, 1)
                    if ahead:
                        make_same(*ahead, 1)
                        penalties(*ahead)
                    dve.wait_ge(exp_turned, n(1, 1))
                    for h in range(2):
                        t = slice(4 * h, 4 * h + 4)
                        v4 = kv[:, b, t, koff:koff + DIM].rearrange("p c (h d) -> p c h d", h=H)
                        e3 = ps[:, 4, 2 * P + 4 * H * h:2 * P + 4 * H * h + 4 * H].rearrange("p (c h) -> p c h", c=4)
                        dve.tensor_copy(kv[:, b, t, koff + DIM:koff + DIM + H], e3)
                        dve.tensor_tensor(v4, v4, bc(e3, dh), ALU.mult).then_inc(msg_done, 1)
                    assert made[0] == links
                steps(dve, body)

            @block.scalar
            def _(act):
                rows = C.sums[:, 0:L.out_width].rearrange("(t p) w -> p t w", p=P)

                def front(j, b):
                    n = at(j, b)
                    if H:
                        act.wait_ge(seg_turned, n(1, 1))
                        act.wait_ge(pen_done, n(1, 0))
                        act.mul(seg_t[:], ps[0:HG, 0, 0:P], BIG).then_inc(seg_copied, 1)
                    for h in range(2 if attr_layer else 0):
                        act.wait_ge(attr_turned, n(2, h + 1))
                        act.wait_ge(attr_mult, n(MULTS, 0))
                        act.copy(attr_t[:, 4 * h:4 * h + 4, :], ps[0:K, 0, :].rearrange("k (c e) -> k c e", c=4)).then_inc(attr_copied, 1)

                def move_products(j, b):
                    per = G // MULTS
                    for m in range(MULTS):
                        act.wait_ge(attr_mult, at(j, b)(MULTS, m + 1))
                        act.copy(attr_sum[:, m * per:m * per + per, :],
                                 ps[:, 1 + m % 2, 0:per * KW].rearrange("p (c w) -> p c w", c=per)).then_inc(attr_moved, 1)

                front(0, 0)
                if MULTS:
                    move_products(0, 0)

                def body(j, b, ahead):
                    n = at(j, b)
                    if ahead and H:
                        front(*ahead)
                    if H:
                        act.wait_ge(below_done, n(1, 1))
                        act.activation(expo[:], below[:], ACT.Exp).then_inc(exp_done, 1)
                    if ahead and MULTS:
                        move_products(*ahead)
                    act.wait_ge(stored[b], j * 16)
                    if H:
                        act.wait_ge(msg_done, n(2, 2))
                        act.copy(outs[:, b, :, MW:MW + H], ps[:, 4, 3 * P:3 * P + HG].rearrange("p (g h) -> p g h", g=G)).then_inc(max_copied, 1)
                    for c in range(G):
                        act.wait_ge(summed[b], j * G + c + 1)
                        act.copy(outs[:, b, c, 0:MW], ps[:, 6 + c % 2, 0:MW]).then_inc(out_free[c % 2], 1)
                    for h in range(2):
                        act.wait_ge(out_free[h], n(4, 4))
                    if H:
                        act.wait_ge(max_copied, n(1, 1))
                    act.dma_start(rows[:, bass.ds(j * (BUFS * G) + b * G, G), :], outs[:, b]).then_inc(stored[b], 16)
                steps(act, body)
                for b in range(BUFS):
                    act.wait_ge(stored[b], ROUNDS * 16)


def combine(nc, C, L, label, target, add):
    H, O, MW, ps = L.heads, L.order, L.msg_width, C.psum
    CW = L.out_width + (1 if H else 0)
    CNT = L.out_width
    dh = DIM // H if H else 0
    with phase(nc, label) as ph:
        conts = ph.sbuf("conts", [P, TB, CW])
        pick = ph.sbuf("pick", [P, TB, P])
        node_id = ph.sbuf("node_id", [P, P])
        home = ph.sbuf("home", [P, L.out_width])
        home_at = ph.sbuf("home_at", [P, 1], I32)
        if H:
            max_row = ph.sbuf("max_row", [H, TB * P])
            run_max = ph.sbuf("run_max", [H, TB * P])
            factor = ph.sbuf("factor", [P, TB, H])
            below = ph.sbuf("below", [P, TB, H])
            small = ph.sbuf("small", [P, 8])
            shift = ph.sbuf("shift", [P, 2 * H])
            most = ph.sbuf("most", [P, H])
            scale = ph.sbuf("scale", [P, 2 * H])
            part = ph.sbuf("part", [P, 2, MW])
            whole = ph.sbuf("whole", [P, MW])
            recip = ph.sbuf("recip", [P, 3, H])

        cleared = ph.sem("cleared")
        conts_in = ph.sem("conts_in")
        max_turned = ph.sem("max_turned")
        row_ready = ph.sem("row_ready")
        conts_scaled = ph.sem("conts_scaled")
        exp_done = ph.sem("exp_done")
        dve_step = ph.sem("dve_step")
        with ph.block() as block:
            first_rows = C.sums[:, 0:L.out_width].rearrange("(t q) w -> q t w", q=P)[0]

            @block.gpsimd
            def _(pool):
                pool.memset(conts[:, TB - 1, :], 0.0).then_inc(cleared, 1)

            @block.sync
            def _(sp):
                sp.wait_ge(cleared, 1)
                sp.dma_start(conts[:, 0:TB - 1, 0:L.out_width],
                             first_rows[0:(TB - 1) * P].rearrange("(b p) w -> p b w", p=P)).then_inc(conts_in, 16)
                sp.dma_start(conts[0:TLAST, TB - 1, 0:L.out_width], first_rows[(TB - 1) * P:T]).then_inc(conts_in, 16)

            @block.tensor
            def _(pe):
                pe.wait_ge(conts_in, 32)
                if not H:
                    return
                for k in range(TB):
                    last = pe.transpose(ps[0:H, k // 4, P * (k % 4):P * (k % 4) + P], conts[:, k, MW:MW + H], C.ident[:])
                last.then_inc(max_turned, 1)
                pe.wait_ge(row_ready, 1)
                for k in range(TB):
                    last = pe.transpose(ps[:, 2, H * k:H * k + H], max_row[:, P * k:P * k + P], C.ident[0:H, 0:H])
                last.then_inc(max_turned, 1)

            @block.scalar
            def _(act):
                if H:
                    act.wait_ge(conts_scaled, 1)
                    act.activation(factor[:], below[:], ACT.Exp).then_inc(exp_done, 1)

            @block.vector
            def _(dve):
                made = [0]

                def link(ins):
                    made[0] += 1
                    ins.then_inc(dve_step, 1)
                    dve.wait_ge(dve_step, made[0])

                dve.tensor_scalar(node_id[:], C.iota[:], 1.0, None, ALU.add)
                if not H:
                    return
                dve.wait_ge(max_turned, 1)
                dve.tensor_copy(max_row[:, 0:512], ps[0:H, 0, :])
                link(dve.tensor_copy(max_row[:, 512:TB * P], ps[0:H, 1, 0:TB * P - 512]))
                link(dve.tensor_tensor_scan(run_max[:], O.cont_pen[0:H, 0:TB * P], max_row[:], -BIG, ALU.add, ALU.max))
                dve.tensor_tensor_scan(max_row[:, ::-1], O.cont_pen[0:H, 1:TB * P + 1][:, ::-1], run_max[:, ::-1], -BIG,
                                       ALU.add, ALU.max).then_inc(row_ready, 1)
                dve.wait_ge(max_turned, 2)
                turned = ps[:, 2, 0:TB * H].rearrange("p (k h) -> p k h", k=TB)
                dve.tensor_tensor(below[:], conts[:, :, MW:MW + H], turned, ALU.subtract).then_inc(conts_scaled, 1)
                dve.wait_ge(conts_scaled, 1)
                link(dve.tensor_copy(conts[:, :, MW:MW + H], turned))
                dve.memset(conts[:, :, CNT:CNT + 1], 1.0)
                dve.wait_ge(exp_done, 1)
                v = conts[:, :, 0:DIM].rearrange("p k (h d) -> p k h d", h=H)
                dve.tensor_tensor(v, v, bc(factor[:], dh), ALU.mult)
                dve.tensor_tensor(conts[:, :, DIM:MW], conts[:, :, DIM:MW], factor[:], ALU.mult)

        home_at_set = ph.sem("home_at_set")
        gathers_begun = ph.sem("gathers_begun")
        home_in = ph.sem("home_in")
        pick_ready = ph.sem("pick_ready")
        conts_summed = ph.sem("conts_summed")
        shift_ready = ph.sem("shift_ready")
        scale_ready = ph.sem("scale_ready")
        merged = ph.sem("merged")
        order_step = ph.sem("order_step")
        with ph.block() as block:
            @block.gpsimd
            def _(pool):
                for b in repeated(pool, NB):
                    pool.wait_ge(merged, b)
                    pool.sem_inc(gathers_begun, 1)
                    pool.tensor_copy(home_at[:], O.home_i[:, bass.ds(b, 1)]).then_inc(home_at_set, 1)
                    pool.wait_ge(home_at_set, b + 1)
                    pool.sem_inc(gathers_begun, 1)
                    pool.indirect_dma_start(home[:], None, C.sums, bass.IndirectOffsetOnAxis(ap=home_at[:], axis=0)
                                            ).then_inc(home_in, 16)

            @block.tensor
            def _(pe):
                for b in repeated(pe, NB):
                    pe.wait_ge(pick_ready, b + 1)
                    pe.wait_ge(merged, b)
                    for k in range(TB):
                        last = pe.matmul(ps[:, 3, 0:CW], pick[:, k, :], conts[:, k, :], start=(k == 0), stop=(k == TB - 1))
                    last.then_inc(conts_summed, 1)

            if H:
                @block.scalar
                def _(act):
                    for b in repeated(act, NB):
                        act.wait_ge(shift_ready, b + 1)
                        act.activation(scale[:], shift[:], ACT.Exp).then_inc(scale_ready, 1)

            @block.vector
            def _(dve):
                links = (11 if add else 10) if H else 1

                def merge(b):
                    made = [0]

                    def link(ins):
                        made[0] += 1
                        ins.then_inc(order_step, 1)
                        dve.wait_ge(order_step, b * links + made[0])

                    dve.wait_ge(conts_summed, b)
                    dve.tensor_tensor(pick[:], node_id[:].unsqueeze(1).to_broadcast([P, TB, P]), bc(O.cont_key[:], P),
                                      ALU.is_equal).then_inc(pick_ready, 1)
                    dve.wait_ge(pick_ready, b + 1)
                    link(dve.tensor_scalar(node_id[:], node_id[:], float(P), None, ALU.add))
                    dve.wait_ge(conts_summed, b + 1)
                    dve.wait_ge(home_in, b * 16 + 16)
                    more = ps[:, 3, :]
                    has = O.has_edges[:, bass.ds(b, 1)]
                    into = target[:, bass.ds(b, 1), :].rearrange("p o w -> p (o w)")
                    if not H:
                        dve.scalar_tensor_tensor(out=into, in0=home[:], scalar=has, in1=more[:, 0:DIM],
                                                 op0=ALU.mult, op1=ALU.add).then_inc(merged, 1)
                        assert made[0] == links
                        return
                    dve.tensor_scalar(small[:, 1:2], more[:, CNT:CNT + 1], 0.0, -BIG, ALU.is_equal, ALU.mult)
                    link(dve.tensor_scalar(small[:, 0:1], more[:, CNT:CNT + 1], 1.0, None, ALU.max))
                    link(dve.reciprocal(small[:, 2:3], small[:, 0:1]))
                    link(dve.tensor_scalar(shift[:, H:2 * H], more[:, MW:MW + H], small[:, 2:3], small[:, 1:2], ALU.mult, ALU.add))
                    link(dve.tensor_tensor(most[:], shift[:, H:2 * H], home[:, MW:MW + H], ALU.max))
                    dve.tensor_tensor(shift[:, 0:H], home[:, MW:MW + H], most[:], ALU.subtract)
                    dve.tensor_tensor(shift[:, H:2 * H], shift[:, H:2 * H], most[:], ALU.subtract).then_inc(shift_ready, 1)
                    dve.wait_ge(scale_ready, b + 1)
                    for s, rows in ((0, home[:, 0:MW]), (1, more[:, 0:MW])):
                        f = scale[:, H * s:H * s + H]
                        dve.tensor_tensor(part[:, s, 0:DIM].rearrange("p (h d) -> p h d", h=H),
                                          rows[:, 0:DIM].rearrange("p (h d) -> p h d", h=H), bc(f, dh), ALU.mult)
                        last = dve.tensor_tensor(part[:, s, DIM:MW], rows[:, DIM:MW], f, ALU.mult)
                    link(last)
                    link(dve.tensor_tensor(whole[:], part[:, 0, :], part[:, 1, :], ALU.add))
                    link(dve.tensor_scalar(recip[:, 0, :], whole[:, DIM:MW], DEN_EPS, None, ALU.add))
                    link(dve.reciprocal(recip[:, 1, :], recip[:, 0, :]))
                    link(dve.tensor_scalar(recip[:, 2, :], recip[:, 1, :], has, None, ALU.mult))
                    w = whole[:, 0:DIM].rearrange("p (h d) -> p h d", h=H)
                    r = bc(recip[:, 2, :], dh)
                    if add:
                        link(dve.tensor_tensor(part[:, 0, 0:DIM].rearrange("p (h d) -> p h d", h=H), w, r, ALU.mult))
                        dve.tensor_tensor(into, into, part[:, 0, 0:DIM], ALU.add).then_inc(merged, 1)
                    else:
                        dve.tensor_tensor(into.rearrange("p (h d) -> p h d", h=H), w, r, ALU.mult).then_inc(merged, 1)
                    assert made[0] == links

                for b in repeated(dve, NB):
                    merge(b)


def layer_norm(nc, C, label, src, dst, affine=None, relu=True):
    with phase(nc, label) as ph:
        square = ph.sbuf("square", [P, NB, DIM])
        stats = ph.sbuf("stats", [P, 4, NB])
        if affine is not None:
            gb = ph.sbuf("gb", [P, 2, DIM])
        vectors_in = ph.sem("vectors_in")
        dve_step = ph.sem("dve_step")
        root_done = ph.sem("root_done")
        with ph.block() as block:
            @block.sync
            def _(sp):
                if affine is not None:
                    for i, v in enumerate(affine):
                        sp.dma_start(gb[:, i, :], v.rearrange("(o n) -> o n", o=1).to_broadcast([P, DIM])).then_inc(vectors_in, 16)

            @block.scalar
            def _(act):
                act.wait_ge(dve_step, 6)
                act.activation(stats[:, 3, :], stats[:, 2, :], ACT.Sqrt).then_inc(root_done, 1)

            @block.vector
            def _(dve):
                made = [0]

                def link(ins):
                    made[0] += 1
                    ins.then_inc(dve_step, 1)
                    dve.wait_ge(dve_step, made[0])

                link(dve.tensor_reduce(stats[:, 0, :], src[:], AX_X, ALU.add))
                link(dve.tensor_scalar(stats[:, 1, :], stats[:, 0, :], 1.0 / DIM, None, ALU.mult))
                link(dve.tensor_tensor(dst[:], src[:], bc(stats[:, 1, :], DIM), ALU.subtract))
                link(dve.tensor_tensor(square[:], dst[:], dst[:], ALU.mult))
                link(dve.tensor_reduce(stats[:, 0, :], square[:], AX_X, ALU.add))
                link(dve.tensor_scalar(stats[:, 2, :], stats[:, 0, :], 1.0 / DIM, LN_EPS, ALU.mult, ALU.add))
                dve.wait_ge(root_done, 1)
                link(dve.reciprocal(stats[:, 0, :], stats[:, 3, :]))
                link(dve.tensor_tensor(dst[:], dst[:], bc(stats[:, 0, :], DIM), ALU.mult))
                if affine is not None:
                    dve.wait_ge(vectors_in, 32)
                    link(dve.tensor_tensor(dst[:], dst[:], gb[:, 0, :].unsqueeze(1).to_broadcast([P, NB, DIM]), ALU.mult))
                    link(dve.tensor_tensor(dst[:], dst[:], gb[:, 1, :].unsqueeze(1).to_broadcast([P, NB, DIM]), ALU.add))
                if relu:
                    dve.tensor_scalar(dst[:], dst[:], 0.0, None, ALU.max)


def project(nc, C, label, src, parts, scales, stores, scores=None):
    ps = C.psum
    total = sum(w.shape[1] for w, _ in parts)
    banks = [(c, min(c + 512, total)) for c in range(0, total, 512)]
    CH = len(banks)
    with phase(nc, label) as ph:
        weight = ph.sbuf("weight", [P, 2, total])
        bias = ph.sbuf("bias", [1, total])
        cur = ph.sbuf("cur", [P, DIM])
        cur_t = ph.sbuf("cur_t", [P, 2, P])
        stage = ph.sbuf("stage", [P, total])
        if scores is not None:
            att = ph.sbuf("att", [P, 2, DIM])
            att_prod = ph.sbuf("att_prod", [P, 2, DIM])
            att_sum = ph.sbuf("att_sum", [P, 2, scores[1]])
        weights_in = ph.sem("weights_in")
        bias_zero = ph.sem("bias_zero")
        cur_ready = ph.sem("cur_ready")
        turned = ph.sem("turned")
        turned_copied = ph.sem("turned_copied")
        mult_done = ph.sem("mult_done")
        staged = ph.sem("staged")
        stored = ph.sem("stored")
        scored = ph.sem("scored")
        evacs = len(scales)
        n_loads = len(parts) + sum(b is not None for _, b in parts) + (2 if scores is not None else 0)
        outs = len(stores(slice(0, P), stage, att_sum if scores is not None else None))
        with ph.block() as block:
            @block.gpsimd
            def _(pool):
                pool.memset(bias[:], 0.0).then_inc(bias_zero, 1)

            @block.sync
            def _(sp):
                sp.wait_ge(bias_zero, 1)
                at = 0
                for w, vec in parts:
                    cols = slice(at, at + w.shape[1])
                    sp.dma_start(weight[:, :, cols], w.rearrange("(k p) n -> p k n", p=P)).then_inc(weights_in, 16)
                    if vec is not None:
                        sp.dma_start(bias[:, cols], vec.rearrange("(o n) -> o n", o=1)).then_inc(weights_in, 16)
                    at += w.shape[1]
                if scores is not None:
                    for i in range(2):
                        sp.dma_start(att[:, i, :], scores[0][i].rearrange("h d -> (h d)").rearrange("(o n) -> o n", o=1)
                                     .to_broadcast([P, DIM])).then_inc(weights_in, 16)
                for b in repeated(sp, NB):
                    sp.wait_ge(staged, b * evacs + evacs)
                    if scores is not None:
                        sp.wait_ge(scored, b * 2 + 2)
                    for dst, src_ap in stores(bass.ds(b * P, P), stage, att_sum if scores is not None else None):
                        sp.dma_start(dst, src_ap).then_inc(stored, 16)
                sp.wait_ge(stored, NB * outs * 16)

            @block.vector
            def _(dve):
                if scores is not None:
                    dve.wait_ge(weights_in, 16 * n_loads)
                for b in repeated(dve, NB):
                    dve.wait_ge(turned, b)
                    dve.tensor_scalar(cur[:], src[:, bass.ds(b, 1), :].rearrange("p o w -> p (o w)"), 1.0, None,
                                      ALU.mult).then_inc(cur_ready, 1)
                    if scores is not None:
                        dve.wait_ge(staged, b * evacs + evacs)
                        dve.wait_ge(stored, b * (outs * 16))
                        dve.tensor_tensor(att_prod[:], stage[:].unsqueeze(1).to_broadcast([P, 2, DIM]), att[:], ALU.mult).then_inc(scored, 1)
                        dve.wait_ge(scored, b * 2 + 1)
                        dve.tensor_reduce(att_sum[:], att_prod[:].rearrange("p s (h d) -> p s h d", h=scores[1]), AX_X,
                                          ALU.add).then_inc(scored, 1)

            @block.tensor
            def _(pe):
                pe.wait_ge(weights_in, 16 * n_loads)
                for b in repeated(pe, NB):
                    pe.wait_ge(cur_ready, b + 1)
                    pe.wait_ge(turned_copied, b)
                    for k in range(2):
                        last = pe.transpose(ps[:, 0, P * k:P * k + P], cur[:, P * k:P * k + P], C.ident[:])
                    last.then_inc(turned, 1)
                    pe.wait_ge(turned_copied, b + 1)
                    pe.wait_ge(staged, b * evacs)
                    for i, (c0, c1) in enumerate(banks):
                        pe.matmul(ps[:, 1 + i, 0:c1 - c0], C.ones[0:1, :], bias[:, c0:c1], start=True, stop=False)
                        for k in range(2):
                            last = pe.matmul(ps[:, 1 + i, 0:c1 - c0], cur_t[:, k, :], weight[:, k, c0:c1], start=False, stop=(k == 1))
                        last.then_inc(mult_done, 1)

            @block.scalar
            def _(act):
                for b in repeated(act, NB):
                    act.wait_ge(turned, b + 1)
                    act.wait_ge(mult_done, b * CH)
                    act.copy(cur_t[:], ps[:, 0, 0:2 * P].rearrange("p (k e) -> p k e", k=2)).then_inc(turned_copied, 1)
                    act.wait_ge(stored, b * (outs * 16))
                    if scores is not None:
                        act.wait_ge(scored, b * 2)
                    for c0, c1, factor in scales:
                        act.wait_ge(mult_done, b * CH + c0 // 512 + 1)
                        act.mul(stage[:, c0:c1], ps[:, 1 + c0 // 512, c0 % 512:c0 % 512 + c1 - c0], factor).then_inc(staged, 1)


def output_projection(nc, C, label, src, into, w_dram, b_dram, alpha_dram):
    ps = C.psum
    with phase(nc, label) as ph:
        weight = ph.sbuf("weight", [P, 2, DIM])
        bias = ph.sbuf("bias", [1, DIM])
        alpha = ph.sbuf("alpha", [P, 1])
        cur = ph.sbuf("cur", [P, DIM])
        cur_t = ph.sbuf("cur_t", [P, 2, P])
        weights_in = ph.sem("weights_in")
        cur_ready = ph.sem("cur_ready")
        turned = ph.sem("turned")
        turned_copied = ph.sem("turned_copied")
        mult_done = ph.sem("mult_done")
        added = ph.sem("added")
        with ph.block() as block:
            @block.sync
            def _(sp):
                sp.dma_start(weight[:], w_dram.rearrange("(k p) n -> p k n", p=P)).then_inc(weights_in, 16)
                sp.dma_start(bias[:], b_dram.rearrange("(o n) -> o n", o=1)).then_inc(weights_in, 16)
                sp.dma_start(alpha[:], alpha_dram.rearrange("(o n) -> o n", o=1).to_broadcast([P, 1])).then_inc(weights_in, 16)

            @block.vector
            def _(dve):
                dve.wait_ge(weights_in, 48)
                for b in repeated(dve, NB):
                    blk = bass.ds(b, 1)
                    dve.wait_ge(turned, b)
                    dve.tensor_scalar(cur[:], src[:, blk, :].rearrange("p o w -> p (o w)"), 1.0, None, ALU.mult).then_inc(cur_ready, 1)
                    dve.wait_ge(mult_done, b + 1)
                    y = into[:, blk, :].rearrange("p o w -> p (o w)")
                    dve.scalar_tensor_tensor(out=y, in0=ps[:, 1, 0:DIM], scalar=alpha[:], in1=y, op0=ALU.mult, op1=ALU.add).then_inc(added, 1)

            @block.tensor
            def _(pe):
                pe.wait_ge(weights_in, 48)
                for b in repeated(pe, NB):
                    pe.wait_ge(cur_ready, b + 1)
                    pe.wait_ge(turned_copied, b)
                    for k in range(2):
                        last = pe.transpose(ps[:, 0, P * k:P * k + P], cur[:, P * k:P * k + P], C.ident[:])
                    last.then_inc(turned, 1)
                    pe.wait_ge(turned_copied, b + 1)
                    pe.wait_ge(added, b)
                    pe.matmul(ps[:, 1, 0:DIM], C.ones[0:1, :], bias[:], start=True, stop=False)
                    for k in range(2):
                        last = pe.matmul(ps[:, 1, 0:DIM], cur_t[:, k, :], weight[:, k, :], start=False, stop=(k == 1))
                    last.then_inc(mult_done, 1)

            @block.scalar
            def _(act):
                for b in repeated(act, NB):
                    act.wait_ge(turned, b + 1)
                    act.wait_ge(mult_done, b)
                    act.copy(cur_t[:], ps[:, 0, 0:2 * P].rearrange("p (k e) -> p k e", k=2)).then_inc(turned_copied, 1)


def feed_forward(nc, C, label, src, y, x, w1, b1, w2, b2, beta_dram):
    ps = C.psum
    FF = w1.shape[1]
    FB = FF // P
    with phase(nc, label) as ph:
        weight1 = ph.sbuf("weight1", [P, 2, FF])
        weight2 = ph.sbuf("weight2", [P, FB, DIM])
        bias1 = ph.sbuf("bias1", [P, FB])
        bias2 = ph.sbuf("bias2", [1, DIM])
        beta = ph.sbuf("beta", [P, 1])
        cur = ph.sbuf("cur", [P, DIM])
        cur_t = ph.sbuf("cur_t", [P, 2, P])
        hidden = ph.sbuf("hidden", [P, FB, P])
        delta = ph.sbuf("delta", [P, DIM])
        weights_in = ph.sem("weights_in")
        cur_ready = ph.sem("cur_ready")
        turned = ph.sem("turned")
        turned_copied = ph.sem("turned_copied")
        hidden_mult = ph.sem("hidden_mult")
        hidden_ready = ph.sem("hidden_ready")
        mult_done = ph.sem("mult_done")
        delta_ready = ph.sem("delta_ready")
        with ph.block() as block:
            @block.sync
            def _(sp):
                sp.dma_start(weight1[:], w1.rearrange("(k p) n -> p k n", p=P)).then_inc(weights_in, 16)
                sp.dma_start(weight2[:], w2.rearrange("(k p) n -> p k n", p=P)).then_inc(weights_in, 16)
                with nc.allow_non_contiguous_dma(reason="a bias per partition"):
                    for f in range(FB):
                        sp.dma_start(bias1[:, f:f + 1], b1[f * P:f * P + P].rearrange("(p o) -> p o", o=1)).then_inc(weights_in, 16)
                sp.dma_start(bias2[:], b2.rearrange("(o n) -> o n", o=1)).then_inc(weights_in, 16)
                sp.dma_start(beta[:], beta_dram.rearrange("(o n) -> o n", o=1).to_broadcast([P, 1])).then_inc(weights_in, 16)

            loads = 16 * (4 + FB)

            @block.vector
            def _(dve):
                dve.wait_ge(weights_in, loads)
                for b in repeated(dve, NB):
                    blk = bass.ds(b, 1)
                    flat = lambda t: t[:, blk, :].rearrange("p o w -> p (o w)")
                    dve.wait_ge(turned, b)
                    dve.tensor_scalar(cur[:], flat(src), 1.0, None, ALU.mult).then_inc(cur_ready, 1)
                    dve.tensor_tensor(flat(x), flat(x), flat(y), ALU.add).then_inc(delta_ready, 1)
                    dve.wait_ge(mult_done, b + 1)
                    dve.wait_ge(delta_ready, b * 2 + 1)
                    dve.scalar_tensor_tensor(out=flat(x), in0=ps[:, 3, 0:DIM], scalar=beta[:], in1=flat(x), op0=ALU.mult,
                                             op1=ALU.add).then_inc(delta_ready, 1)

            @block.tensor
            def _(pe):
                pe.wait_ge(weights_in, loads)
                for b in repeated(pe, NB):
                    pe.wait_ge(cur_ready, b + 1)
                    for k in range(2):
                        last = pe.transpose(ps[:, 0, P * k:P * k + P], cur[:, P * k:P * k + P], C.ident[:])
                    last.then_inc(turned, 1)
                    pe.wait_ge(turned_copied, b + 1)
                    for f in range(FB):
                        if f % 4 == 0:
                            pe.wait_ge(hidden_ready, b * FB)
                        for k in range(2):
                            last = pe.matmul(ps[:, 1 + f // 4, P * (f % 4):P * (f % 4) + P], weight1[:, k, f * P:f * P + P],
                                             cur_t[:, k, :], start=(k == 0), stop=(k == 1))
                        if f % 4 == 3:
                            last.then_inc(hidden_mult, 1)
                    pe.wait_ge(delta_ready, b * 2)
                    pe.matmul(ps[:, 3, 0:DIM], C.ones[0:1, :], bias2[:], start=True, stop=False)
                    for f in range(FB):
                        pe.wait_ge(hidden_ready, b * FB + f + 1)
                        last = pe.matmul(ps[:, 3, 0:DIM], hidden[:, f, :], weight2[:, f, :], start=False, stop=(f == FB - 1))
                    last.then_inc(mult_done, 1)

            @block.scalar
            def _(act):
                act.wait_ge(weights_in, loads)
                for b in repeated(act, NB):
                    act.wait_ge(turned, b + 1)
                    act.copy(cur_t[:], ps[:, 0, 0:2 * P].rearrange("p (k e) -> p k e", k=2)).then_inc(turned_copied, 1)
                    act.wait_ge(mult_done, b)
                    for f in range(FB):
                        if f % 4 == 0:
                            act.wait_ge(hidden_mult, b * 2 + f // 4 + 1)
                        act.activation(hidden[:, f, :], ps[:, 1 + f // 4, P * (f % 4):P * (f % 4) + P], ACT.Gelu,
                                       bias=bias1[:, f:f + 1]).then_inc(hidden_ready, 1)


def batch_norm(nc, C, label, agg, x, gamma_dram, beta_dram):
    ps = C.psum
    with phase(nc, label) as ph:
        square = ph.sbuf("square", [P, NB, DIM])
        valid = ph.sbuf("valid", [P, 1])
        vecs = ph.sbuf("vecs", [P, 2, DIM])
        mean = ph.sbuf("mean", [P, DIM])
        var = ph.sbuf("var", [P, DIM])
        root = ph.sbuf("root", [P, DIM])
        coef = ph.sbuf("coef", [P, 2, DIM])
        valid_set = ph.sem("valid_set")
        vecs_in = ph.sem("vecs_in")
        dve_step = ph.sem("dve_step")
        summed = ph.sem("summed")
        root_done = ph.sem("root_done")
        with ph.block() as block:
            @block.gpsimd
            def _(pool):
                pool.memset(valid[:], 1.0).then_inc(valid_set, 1)
                pool.wait_ge(valid_set, 1)
                pool.affine_select(out=valid[:], in_=valid[:], compare_op=ALU.is_gt, fill=0.0, base=LAST,
                                   pattern=[[0, 1]], channel_multiplier=-1).then_inc(valid_set, 1)

            @block.sync
            def _(sp):
                for i, v in enumerate((gamma_dram, beta_dram)):
                    sp.dma_start(vecs[:, i, :], v.rearrange("(o n) -> o n", o=1).to_broadcast([P, DIM])).then_inc(vecs_in, 16)

            @block.tensor
            def _(pe):
                for i, tile in enumerate((agg, square)):
                    pe.wait_ge(dve_step, (1, 5)[i])
                    for b in range(NB):
                        last = pe.matmul(ps[:, i, 0:DIM], C.ones[:], tile[:, b, :], start=(b == 0), stop=(b == NB - 1))
                    last.then_inc(summed, 1)

            @block.scalar
            def _(act):
                act.wait_ge(dve_step, 6)
                act.activation(root[:], var[:], ACT.Sqrt).then_inc(root_done, 1)

            @block.vector
            def _(dve):
                made = [0]

                def link(ins):
                    made[0] += 1
                    ins.then_inc(dve_step, 1)
                    dve.wait_ge(dve_step, made[0])

                last_block = agg[:, NB - 1, :]
                wide = lambda t: t.unsqueeze(1).to_broadcast([P, NB, DIM])
                dve.wait_ge(valid_set, 2)
                link(dve.tensor_scalar(last_block, last_block, valid[:], None, ALU.mult))
                dve.wait_ge(summed, 1)
                link(dve.tensor_scalar(mean[:], ps[:, 0, 0:DIM], 1.0 / N, None, ALU.mult))
                link(dve.tensor_tensor(agg[:], agg[:], wide(mean[:]), ALU.subtract))
                link(dve.tensor_scalar(last_block, last_block, valid[:], None, ALU.mult))
                link(dve.tensor_tensor(square[:], agg[:], agg[:], ALU.mult))
                dve.wait_ge(summed, 2)
                link(dve.tensor_scalar(var[:], ps[:, 1, 0:DIM], 1.0 / N, LN_EPS, ALU.mult, ALU.add))
                dve.wait_ge(root_done, 1)
                link(dve.reciprocal(coef[:, 0, :], root[:]))
                dve.wait_ge(vecs_in, 32)
                link(dve.tensor_tensor(coef[:, 1, :], coef[:, 0, :], vecs[:, 0, :], ALU.mult))
                link(dve.tensor_tensor(agg[:], agg[:], wide(coef[:, 1, :]), ALU.mult))
                link(dve.tensor_tensor(agg[:], agg[:], wide(vecs[:, 1, :]), ALU.add))
                dve.tensor_tensor(x[:], x[:], agg[:], ALU.add)


def load_x(nc, C, x_dram, x):
    with phase(nc, "load_x") as ph:
        cleared, loaded = ph.sem("cleared"), ph.sem("loaded")
        with ph.block() as block:
            @block.gpsimd
            def _(pool):
                pool.memset(x[:, NB - 1, :], 0.0).then_inc(cleared, 1)

            @block.sync
            def _(sp):
                full = (NB - 1) * P
                sp.dma_start(x[:, 0:NB - 1, :], x_dram[0:full].rearrange("(b p) w -> p b w", p=P)).then_inc(loaded, 16)
                sp.wait_ge(cleared, 1)
                sp.dma_start(x[0:LAST, NB - 1, :], x_dram[full:N]).then_inc(loaded, 16)
                sp.wait_ge(loaded, 32)


def store_out(nc, C, x, bias_dram, out):
    with phase(nc, "store_out") as ph:
        bias = ph.sbuf("bias", [P, DIM])
        bias_in, added, stored = ph.sem("bias_in"), ph.sem("added"), ph.sem("stored")
        with ph.block() as block:
            @block.vector
            def _(dve):
                dve.wait_ge(bias_in, 16)
                dve.tensor_tensor(x[:], x[:], bias[:].unsqueeze(1).to_broadcast([P, NB, DIM]), ALU.add).then_inc(added, 1)

            @block.sync
            def _(sp):
                full = (NB - 1) * P
                sp.dma_start(bias[:], bias_dram.rearrange("(o n) -> o n", o=1).to_broadcast([P, DIM])).then_inc(bias_in, 16)
                sp.wait_ge(added, 1)
                sp.dma_start(out[0:full].rearrange("(b p) w -> p b w", p=P), x[:, 0:NB - 1, :]).then_inc(stored, 16)
                sp.dma_start(out[full:N], x[0:LAST, NB - 1, :]).then_inc(stored, 16)
                sp.wait_ge(stored, 32)


def build(nc, A, out):
    with ExitStack() as ctx:
        C = make_constants(nc, ctx)
        by_src = make_order(nc, ctx, "by_src", 18, 24)
        by_dst = make_order(nc, ctx, "by_dst", 64, 72)
        x = ctx.enter_context(nc.sbuf_tensor("x", [P, NB, DIM], F32))

        def table(name, rows, cols):
            return nc.dram_tensor(name, (rows, cols), F32, kind="Internal").ap()

        build_constants(nc, C)
        load_x(nc, C, A["x"], x)
        sort_edges(nc, C, by_src, "sort_src", A["src"], A["dst"], A["edge_attr_18"], None, None)
        sort_edges(nc, C, by_dst, "sort_dst", A["dst"], A["src"], A["edge_attr_64"], A["edge_type_8"], A["edge_weight"])

        H0 = 16
        q0, kv0 = table("q0", NR, P), table("kv0", NR, P + DIM)
        w = A["L0_gnn_Wqkv"]
        with nc.sbuf_tensor("h0", [P, NB, DIM], F32) as h:
            layer_norm(nc, C, "norm0", x, h)
            project(nc, C, "tables0", h, [(w, A["L0_gnn_bqkv"])],
                    [(0, P, (P // H0) ** -0.5), (P, 2 * P + DIM, 1.0)],
                    lambda rows, stage, sums: [(q0[rows, :], stage[:, 0:P]), (kv0[rows, :], stage[:, P:])])
        L = Layer(0, H0, by_src, P, P + DIM, P)
        C.sums = table("sums0", EP, L.out_width)
        edge_layer(nc, C, L, "edges0", (kv0, q0),
                   [(A["L0_gnn_Wk_rpe"], A["L0_gnn_bk_rpe"]), (A["L0_gnn_Wq_rpe"], A["L0_gnn_bq_rpe"])])
        combine(nc, C, L, "combine0", x, True)

        H1 = 8
        q1, kv1 = table("q1", NR, DIM), table("kv1", NR, 2 * DIM)
        with nc.sbuf_tensor("h1", [P, NB, DIM], F32) as h:
            layer_norm(nc, C, "norm1", x, h)
            with nc.sbuf_tensor("hn1", [P, NB, DIM], F32) as hn:
                layer_norm(nc, C, "norm1a", h, hn, (A["L1_gnn_ln1_g"], A["L1_gnn_ln1_b"]), relu=False)
                project(nc, C, "tables1", hn, [(A[f"L1_gnn_W{c}"], A[f"L1_gnn_b{c}"]) for c in "qkv"],
                        [(0, DIM, (DIM // H1) ** -0.5), (DIM, 2 * DIM, 1.0), (2 * DIM, 3 * DIM, 1.0)],
                        lambda rows, stage, sums: [(q1[rows, :], stage[:, 0:DIM]), (kv1[rows, :], stage[:, DIM:])])
            L = Layer(1, H1, by_dst, DIM, 2 * DIM, DIM)
            C.sums = table("sums1", EP, L.out_width)
            edge_layer(nc, C, L, "edges1", (kv1, q1), [(A["L1_gnn_We"], A["L1_gnn_be"])])
            with nc.sbuf_tensor("att1", [P, NB, DIM], F32) as att:
                combine(nc, C, L, "combine1", att, False)
                output_projection(nc, C, "out_proj1", att, h, A["L1_gnn_Wo"], A["L1_gnn_bo"], A["L1_gnn_alpha"])
                layer_norm(nc, C, "norm1b", h, att, (A["L1_gnn_ln2_g"], A["L1_gnn_ln2_b"]), relu=False)
                feed_forward(nc, C, "ff1", att, h, x, A["L1_gnn_W1"], A["L1_gnn_b1"], A["L1_gnn_W2"], A["L1_gnn_b2"],
                             A["L1_gnn_beta"])

        R = A["L2_gnn_weight"].shape[0]
        rel = table("rel2", NR * R, DIM)
        with nc.sbuf_tensor("h2", [P, NB, DIM], F32) as h:
            layer_norm(nc, C, "norm2", x, h)
            wide_rel = rel.rearrange("(n r) w -> n (r w)", r=R)
            project(nc, C, "tables2", h, [(A["L2_gnn_weight"][r], None) for r in range(R)],
                    [(c, c + 512, 1.0) for c in range(0, R * DIM, 512)],
                    lambda rows, stage, sums: [(wide_rel[rows, :], stage[:])])
        L = Layer(2, 0, by_dst, 0, DIM, 0)
        C.sums = table("sums2", EP, L.out_width)
        edge_layer(nc, C, L, "edges2", (rel,), [])
        with nc.sbuf_tensor("agg2", [P, NB, DIM], F32) as agg:
            combine(nc, C, L, "combine2", agg, False)
            batch_norm(nc, C, "batch_norm2", agg, x, A["L2_gnn_gamma"], A["L2_gnn_beta"])

        H3 = A["L3_gnn_attn_l"].shape[0]
        feat, right = table("feat3", NR, H3 + DIM), table("right3", NR, H3)
        with nc.sbuf_tensor("h3", [P, NB, DIM], F32) as h:
            layer_norm(nc, C, "norm3", x, h)
            project(nc, C, "tables3", h, [(A["L3_gnn_W"], None)], [(0, DIM, 1.0)],
                    lambda rows, stage, sums: [(feat[rows, H3:], stage[:]), (feat[rows, 0:H3], sums[:, 0, :]), (right[rows, :], sums[:, 1, :])],
                    scores=((A["L3_gnn_attn_l"], A["L3_gnn_attn_r"]), H3))
        L = Layer(3, H3, by_dst, H3, H3 + DIM, H3)
        C.sums = table("sums3", EP, L.out_width)
        edge_layer(nc, C, L, "edges3", (feat, right), [])
        combine(nc, C, L, "combine3", x, True)
        store_out(nc, C, x, A["L3_gnn_bias"], out)


_INS = ["x", "src", "dst", "edge_attr_18", "edge_attr_64", "edge_type_8", "edge_weight",
        "L0_gnn_Wqkv", "L0_gnn_bqkv", "L0_gnn_Wk_rpe", "L0_gnn_bk_rpe", "L0_gnn_Wq_rpe", "L0_gnn_bq_rpe",
        "L1_gnn_Wq", "L1_gnn_bq", "L1_gnn_Wk", "L1_gnn_bk", "L1_gnn_Wv", "L1_gnn_bv", "L1_gnn_We", "L1_gnn_be",
        "L1_gnn_Wo", "L1_gnn_bo", "L1_gnn_ln1_g", "L1_gnn_ln1_b", "L1_gnn_ln2_g", "L1_gnn_ln2_b",
        "L1_gnn_W1", "L1_gnn_b1", "L1_gnn_W2", "L1_gnn_b2", "L1_gnn_alpha", "L1_gnn_beta",
        "L2_gnn_weight", "L2_gnn_gamma", "L2_gnn_beta", "L3_gnn_W", "L3_gnn_attn_l", "L3_gnn_attn_r", "L3_gnn_bias"]


def kernel(**inputs):
    import numpy as _np
    import concourse.bacc as _bacc
    from concourse import mybir as _mybir
    from concourse.bass_utils import run_bass_kernel_spmd as _run

    nc = _bacc.Bacc("TRN2", target_bir_lowering=False, num_devices=1)
    arrays, args = {}, {}
    for name in _INS:
        a = _np.ascontiguousarray(inputs[name])
        arrays[f"in_{name}_dram"] = a
        args[name] = nc.dram_tensor(f"in_{name}_dram", a.shape, _mybir.dt.from_np(a.dtype), kind="ExternalInput").ap()
    out = nc.dram_tensor("out_dram", (N, DIM), F32, kind="ExternalOutput").ap()
    build(nc, args, out)
    r = _run(nc, [arrays], core_ids=[0])
    return r.results[0]["out_dram"]
```

```python
from contextlib import ExitStack, contextmanager

import concourse.bass as bass
from concourse import mybir

F32 = mybir.dt.float32
BF16 = mybir.dt.bfloat16
I32 = mybir.dt.int32
ALU = mybir.AluOpType
ACT = mybir.ActivationFunctionType
AX_X = mybir.AxisListType.X

P = 128
N, DIM, E = 3125, 256, 103125
NB = -(-N // P)
NR = NB * P
LAST = N - (NB - 1) * P
G = 8
T = 816
STEPS = T // G
BUFS = (3, 3, 3, 6)
EP = T * P
TB = -(-T // P)
TLAST = T - (TB - 1) * P
MAIN = 800
REST = E - MAIN * P
RCOL, RLAST = REST // P, REST % P
BIG = 1e30
DEN_EPS = 1e-16
LN_EPS = 1e-5
WP = DIM + 32

ONE, SEG, KEY, IDX, IDX_REL, WEIGHT = range(6)
SPREAD = 8
SPREAD_W = 4


class Order:

    def __init__(self, attrs, width):
        self.attrs, self.width = attrs, width


class Layer:
    def __init__(self, kind, heads, order, q_width, kv_width, koff):
        self.kind, self.heads, self.order = kind, heads, order
        self.q_width, self.kv_width, self.koff = q_width, kv_width, koff
        self.out_width = DIM + 2 * heads
        self.msg_width = DIM + heads


@contextmanager
def phase(nc, label):
    sems = []

    with ExitStack() as ctx:
        class Ph:
            @staticmethod
            def sbuf(name, shape, dt=F32):
                return ctx.enter_context(nc.sbuf_tensor(f"{label}_{name}", shape, dt))

            @staticmethod
            def sem(name):
                s = nc.alloc_semaphore(f"{label}_{name}")
                sems.append(s)
                return s

            @staticmethod
            def block():
                return nc.Block()
        yield Ph
        nc.clear_and_free_semaphores(sems)
        nc.all_engine_barrier()


def bc(ap, n):
    return ap.unsqueeze(len(ap.shape)).to_broadcast([*ap.shape, n])


def repeated(eng, count):
    yield 0
    with eng.Fori(1, count) as step:
        yield step


def build_constants(nc, C):
    with phase(nc, "const") as ph:
        pool_step = ph.sem("pool_step")
        with ph.block() as block:
            @block.gpsimd
            def _(pool):
                n = [0]

                def link(ins):
                    n[0] += 1
                    ins.then_inc(pool_step, 1)
                    pool.wait_ge(pool_step, n[0])

                for ident in (C.ident, C.ident_b):
                    link(pool.memset(ident[:], 0.0))
                    link(pool.affine_select(out=ident[:], in_=ident[:], compare_op=ALU.not_equal, fill=1.0,
                                            base=0, pattern=[[-1, P]], channel_multiplier=1))
                for tri, sign in ((C.lower, 1), (C.upper, -1)):
                    link(pool.memset(tri[:], 1.0))
                    link(pool.affine_select(out=tri[:], in_=tri[:], compare_op=ALU.is_gt, fill=0.0,
                                            base=0, pattern=[[-sign, P]], channel_multiplier=sign))
                link(pool.memset(C.ones[:], 1.0))
                link(pool.memset(C.zeros[:], 0.0))
                link(pool.memset(C.zeros_b[:], 0.0))
                link(pool.iota(C.iota_i[:], pattern=[[1, P]], base=0, channel_multiplier=0))
                link(pool.tensor_copy(C.iota[:], C.iota_i[:]))
                link(pool.tensor_copy(C.iota_b[:], C.iota[:]))


def sort_edges(nc, C, O, label, key_dram, other_dram, attr_dram, type_dram, weight_dram):
    A, W = O.attrs, O.width
    rel = type_dram is not None
    ps = C.psum
    with phase(nc, label) as ph:
        key_i = ph.sbuf("key_i", [P, T], I32)
        idx_i = ph.sbuf("idx_i", [P, T], I32)
        hi_i = ph.sbuf("hi_i", [P, T], I32)
        lo_i = ph.sbuf("lo_i", [P, T], I32)
        hi_b = ph.sbuf("hi_b", [P, T], BF16)
        lo_b = ph.sbuf("lo_b", [P, T], BF16)
        seg_f = ph.sbuf("seg_f", [P, T])
        if rel:
            type_i = ph.sbuf("type_i", [P, T], I32)
            rel_i = ph.sbuf("rel_i", [P, T], I32)
            weight = ph.sbuf("weight", [P, T])
        hot_hi = ph.sbuf("hot_hi", [P, 2, G, NB], BF16)
        hot_lo = ph.sbuf("hot_lo", [P, 2, G, P], BF16)
        hot_hi_t = ph.sbuf("hot_hi_t", [NB, 2, G, P])
        hist = ph.sbuf("hist", [NB, P])
        cum = ph.sbuf("cum", [NB, P])
        before_row = ph.sbuf("before_row", [NB, 1])
        starts = ph.sbuf("starts", [NB, P])
        table = ph.sbuf("table", [NB, 2, P])
        junk = ph.sbuf("junk", [P, 2, G, P], BF16)
        base = ph.sbuf("base", [P, 2, G])
        rank = ph.sbuf("rank", [P, 2, G])
        pos_i = ph.sbuf("pos_i", [P, 2, G], I32)
        rec = ph.sbuf("rec", [P, 2, G, W])
        reci = rec[:].bitcast(I32)
        key_cur = ph.sbuf("key_cur", [P, 2, G])
        halves = ph.sbuf("halves", [P, 2, G, 2], BF16)
        ident_hi = ph.sbuf("ident_hi", [P, P], BF16)
        seg_prev = ph.sbuf("seg_prev", [P, TB])
        seg_head = ph.sbuf("seg_head", [P, TB])

        filled = ph.sem("filled")
        loaded = ph.sem("loaded")
        dve_step = ph.sem("dve_step")
        split = ph.sem("split")
        hist_ready = ph.sem("hist_ready")
        hist_used = [ph.sem(f"hist_used{b}") for b in range(2)]
        sums = ph.sem("sums")
        starts_ready = ph.sem("starts_ready")
        with ph.block() as block:
            loads = [(key_i, key_dram), (idx_i, other_dram)]
            if rel:
                loads += [(type_i, type_dram), (weight, weight_dram)]

            @block.gpsimd
            def _(pool):
                pool.memset(key_i[:], N).then_inc(filled, 1)
                pool.memset(idx_i[:], N).then_inc(filled, 1)
                if rel:
                    pool.memset(type_i[:], 0).then_inc(filled, 1)
                    pool.memset(weight[:], 0.0).then_inc(filled, 1)
                pool.memset(rec[:], 0.0).then_inc(filled, 1)
                pool.memset(seg_prev[:], 0.0).then_inc(filled, 1)
                pool.memset(seg_head[:], 0.0).then_inc(filled, 1)

            @block.sync
            def _(sp):
                sp.wait_ge(filled, len(loads) + 3)
                for tile, dram in loads:
                    sp.dma_start(tile[:, 0:MAIN], dram[0:MAIN * P].rearrange("(p j) -> p j", j=MAIN)).then_inc(loaded, 16)
                    rest = dram[MAIN * P:MAIN * P + RCOL * P].rearrange("(g p o) -> g p o", p=P, o=1)
                    for g in range(RCOL):
                        sp.dma_start(tile[:, MAIN + g:MAIN + g + 1], rest[g]).then_inc(loaded, 16)
                    sp.dma_start(tile[0:RLAST, MAIN + RCOL:MAIN + RCOL + 1],
                                 dram[E - RLAST:E].rearrange("(p o) -> p o", o=1)).then_inc(loaded, 16)

            @block.vector
            def _(dve):
                n = [0]

                def link(ins):
                    n[0] += 1
                    ins.then_inc(dve_step, 1)
                    dve.wait_ge(dve_step, n[0])

                dve.wait_ge(loaded, 16 * len(loads) * (RCOL + 2))
                link(dve.tensor_scalar(hi_i[:], key_i[:], 7, None, ALU.arith_shift_right))
                link(dve.tensor_scalar(lo_i[:], key_i[:], P - 1, None, ALU.bitwise_and))
                link(dve.tensor_copy(hi_b[:], hi_i[:]))
                link(dve.tensor_copy(lo_b[:], lo_i[:]))
                link(dve.tensor_scalar(ident_hi[:], C.ident_b[:], float(P), None, ALU.mult))
                link(dve.tensor_scalar(seg_f[:], key_i[:], 1.0, None, ALU.add))
                if rel:
                    link(dve.scalar_tensor_tensor(out=rel_i[:], in0=idx_i[:], scalar=8.0, in1=type_i[:],
                                                  op0=ALU.mult, op1=ALU.add))
                dve.memset(rec[:, :, :, A + ONE:A + ONE + 1], 1.0)

        with ph.block() as block:
            @block.vector
            def _(dve):
                for j in repeated(dve, STEPS // 2):
                    for b in range(2):
                        dve.wait_ge(hist_used[b], j)
                        cols = bass.ds(j * (2 * G) + b * G, G)
                        dve.tensor_tensor(hot_hi[:, b], C.iota_b[:, 0:NB].unsqueeze(1).to_broadcast([P, G, NB]),
                                          bc(hi_b[:, cols], NB), ALU.is_equal).then_inc(hist_ready, 1)
                        dve.tensor_tensor(hot_lo[:, b], C.iota_b[:].unsqueeze(1).to_broadcast([P, G, P]),
                                          bc(lo_b[:, cols], P), ALU.is_equal).then_inc(hist_ready, 1)

                dve.wait_ge(sums, 1)
                dve.tensor_copy(hist[:], ps[0:NB, 0, 0:P]).then_inc(dve_step, 1)
                done = 7 + rel
                dve.wait_ge(dve_step, done)
                dve.tensor_tensor_scan(cum[:], C.ones[0:NB, :], hist[:], 0.0, ALU.mult, ALU.add).then_inc(starts_ready, 1)
                dve.wait_ge(sums, 2)
                dve.tensor_copy(before_row[:], ps[0:NB, 1, 0:1]).then_inc(dve_step, 1)
                dve.wait_ge(dve_step, done + 1)
                dve.scalar_tensor_tensor(out=starts[:], in0=cum[:], scalar=before_row[:], in1=hist[:],
                                         op0=ALU.add, op1=ALU.subtract).then_inc(starts_ready, 1)
                dve.wait_ge(sums, 3)
                dve.tensor_scalar(O.home_i[:], ps[:, 2, 0:NB], float(EP - 1), None, ALU.min)
                dve.tensor_scalar(O.has_edges[:], ps[:, 2, P:P + NB], 0.0, None, ALU.is_gt)

            @block.tensor
            def _(pe):
                pe.matmul(ps[0:NB, 0, 0:P], C.zeros_b[:, 0:NB], C.zeros_b[:], start=True, stop=False,
                          skip_group_check=True)
                for j in repeated(pe, STEPS // 2):
                    for b in range(2):
                        pe.wait_ge(hist_ready, j * 4 + 2 * b + 2)
                        for c in range(G):
                            last = pe.matmul(ps[0:NB, 0, 0:P], hot_hi[:, b, c, :], hot_lo[:, b, c, :],
                                             start=False, stop=False, skip_group_check=True)
                        last.then_inc(hist_used[b], 1)
                pe.matmul(ps[0:NB, 0, 0:P], C.zeros_b[:, 0:NB], C.zeros_b[:], start=False, stop=True,
                          skip_group_check=True).then_inc(sums, 1)
                pe.wait_ge(starts_ready, 1)
                pe.matmul(ps[0:NB, 1, 0:1], C.upper[0:NB, 0:NB], cum[:, P - 1:P], start=True, stop=True).then_inc(sums, 1)
                pe.wait_ge(starts_ready, 2)
                pe.transpose(ps[:, 2, 0:NB], starts[:], C.ident[0:NB, 0:NB])
                pe.transpose(ps[:, 2, P:P + NB], hist[:], C.ident[0:NB, 0:NB]).then_inc(sums, 1)

        hot_ready = ph.sem("hot_ready")
        seg_ready = ph.sem("seg_ready")
        words_ready = ph.sem("words_ready")
        attrs_in = [ph.sem(f"attrs_in{b}") for b in range(2)]
        turned = ph.sem("turned")
        turned_copied = ph.sem("turned_copied")
        keys_ready = ph.sem("keys_ready")
        ranked = ph.sem("ranked")
        table_ready = ph.sem("table_ready")
        looked_up = ph.sem("looked_up")
        row_used = [ph.sem(f"row_used{b}") for b in range(2)]
        table_moved = ph.sem("table_moved")
        pos_ready = ph.sem("pos_ready")
        scattered = [ph.sem(f"scattered{b}") for b in range(2)]
        scatters_begun = ph.sem("scatters_begun")
        words_begun = ph.sem("words_begun")
        with ph.block() as block:
            attr_main = attr_dram[0:MAIN * P, :].rearrange("(p j) a -> p j a", j=MAIN)

            def at(j, b):
                return lambda k, o: j * (2 * k) + (b * k + o)

            def steps(eng, body):
                for j in repeated(eng, MAIN // G // 2):
                    body(j, 0, (j, 1), False)
                    body(j, 1, (j + 1, 0), False)
                j = MAIN // G // 2
                body(j, 0, (j, 1), True)
                body(j, 1, None, True)

            @block.sync
            def _(sp):
                def body(j, b, ahead, tail):
                    sp.wait_ge(scattered[b], j * P)
                    if not tail:
                        sp.dma_start(rec[:, b, :, 0:A], attr_main[:, bass.ds(j * (2 * G) + b * G, G), :]).then_inc(attrs_in[b], 16)
                    elif b == 0:
                        sp.dma_start(rec[:, b, 0:RCOL, 0:A],
                                     attr_dram[MAIN * P:MAIN * P + RCOL * P, :].rearrange("(g p) a -> p g a", p=P)).then_inc(attrs_in[b], 16)
                        sp.dma_start(rec[0:RLAST, b, RCOL, 0:A], attr_dram[E - RLAST:E, :]).then_inc(attrs_in[b], 16)
                steps(sp, body)

            @block.gpsimd
            def _(pool):
                def body(j, b, ahead, tail):
                    pool.wait_ge(words_ready, j * 2 + b + 1)
                    pool.wait_ge(attrs_in[b], (j + (2 if tail and b == 0 else 0 if tail else 1)) * 16)
                    pool.wait_ge(pos_ready, j * 2 + b + 1)
                    pool.sem_inc(scatters_begun, 1)
                    for c in range(G):
                        pool.indirect_dma_start(O.rec, bass.IndirectOffsetOnAxis(ap=pos_i[:, b, c:c + 1], axis=0),
                                                rec[:, b, c, :], None).then_inc(scattered[b], 16)
                steps(pool, body)
                for b in range(2):
                    pool.wait_ge(scattered[b], (STEPS // 2) * P)

            @block.scalar
            def _(act):
                act.copy(table[:, 0, :], starts[:]).then_inc(table_ready, 1)

                def keys(j, b):
                    cols = bass.ds(j * (2 * G) + b * G, G)
                    act.copy(key_cur[:, b, :], key_i[:, cols])
                    act.copy(halves[:, b, :, 0], hi_b[:, cols])
                    act.copy(halves[:, b, :, 1], lo_b[:, cols]).then_inc(seg_ready, 1)

                def turn(j, b, h):
                    act.wait_ge(turned, at(j, b)(2, h + 1))
                    act.copy(hot_hi_t[:, b, 4 * h:4 * h + 4, :], ps[0:NB, h, :].rearrange("k (c e) -> k c e", c=4)).then_inc(turned_copied, 1)

                keys(0, 0)
                turn(0, 0, 0)
                turn(0, 0, 1)

                def body(j, b, ahead, tail):
                    n = at(j, b)
                    cols = bass.ds(j * (2 * G) + b * G, G)
                    for c in range(G):
                        act.wait_ge(table_moved, n(G, c + 1))
                        act.copy(table[:, (c + 1) % 2, :], ps[0:NB, 6, 0:P]).then_inc(table_ready, 1)
                        if ahead and c == 2:
                            if not (isinstance(j, int) and j == 0 and b == 0):
                                act.wait_ge(pos_ready, n(1, 0))
                            keys(*ahead)
                        if ahead and c in (5, 6):
                            turn(*ahead, c - 5)
                    words = [(SEG, seg_f, rec), (KEY, key_i, reci), (IDX, idx_i, reci)]
                    if rel:
                        words += [(IDX_REL, rel_i, reci), (WEIGHT, weight, rec)]
                    act.wait_ge(scattered[b], j * P)
                    act.sem_inc(words_begun, 1)
                    for w, src, dst in words:
                        last = act.copy(dst[:, b, :, A + w], src[:, cols])
                    last.then_inc(words_ready, 1)
                steps(act, body)

            @block.vector
            def _(dve):
                def one_hots(j, b):
                    cols = bass.ds(j * (2 * G) + b * G, G)
                    dve.tensor_tensor(hot_hi[:, b], C.iota_b[:, 0:NB].unsqueeze(1).to_broadcast([P, G, NB]),
                                      bc(hi_b[:, cols], NB), ALU.is_equal).then_inc(hot_ready, 1)
                    dve.tensor_tensor(hot_lo[:, b], C.iota_b[:].unsqueeze(1).to_broadcast([P, G, P]),
                                      bc(lo_b[:, cols], P), ALU.is_equal).then_inc(hot_ready, 1)

                one_hots(0, 0)

                def body(j, b, ahead, tail):
                    n = at(j, b)
                    for h in range(2):
                        dve.wait_ge(keys_ready, n(2, h + 1))
                        for c in range(4 * h, 4 * h + 4):
                            last = dve.scalar_tensor_tensor(out=junk[:, 0, c], in0=ps[:, 4 + h, P * (c % 4):P * (c % 4) + P],
                                                            scalar=key_cur[:, b, c:c + 1], in1=C.lower[:],
                                                            op0=ALU.is_equal, op1=ALU.mult, accum_out=rank[:, b, c:c + 1])
                        last.then_inc(ranked, 1)
                        for c in range(4 * h, 4 * h + 4):
                            dve.wait_ge(looked_up, n(G, c + 1))
                            dve.scalar_tensor_tensor(out=junk[:, 1, c], in0=ps[:, 2 + c % 2, 0:P], scalar=1.0,
                                                     in1=hot_lo[:, b, c, :], op0=ALU.mult, op1=ALU.mult,
                                                     accum_out=base[:, b, c:c + 1]).then_inc(row_used[c % 2], 1)
                            if c == 1 and ahead:
                                one_hots(*ahead)
                    dve.wait_ge(ranked, n(2, 2))
                    for h in range(2):
                        dve.wait_ge(row_used[h], n(4, 4))
                    dve.wait_ge(scattered[b], j * P)
                    dve.tensor_tensor(pos_i[:, b, :], base[:, b, :], rank[:, b, :], ALU.add).then_inc(pos_ready, 1)
                steps(dve, body)

            @block.tensor
            def _(pe):
                pe.matmul(ps[0:NB, 6, 0:P], C.ident[0:NB, 0:NB], starts[:], start=True, stop=False, skip_group_check=True)

                def turn(j, b, h):
                    pe.wait_ge(hot_ready, at(j, b)(2, 2))
                    for c in range(4):
                        last = pe.matmul(ps[0:NB, h, P * c:P * c + P], hot_hi[:, b, 4 * h + c, :], C.ident_b[:],
                                         start=True, stop=True)
                    last.then_inc(turned, 1)

                def keys(j, b, h, first=False):
                    pe.wait_ge(seg_ready, at(j, b)(1, 1))
                    if not first:
                        pe.wait_ge(ranked, at(j, b)(2, h) - 1)
                    for c in range(4):
                        for i, rows in enumerate((ident_hi, C.ident_b)):
                            last = pe.matmul(ps[:, 4 + h, P * c:P * c + P], halves[:, b, 4 * h + c, i:i + 1].to_broadcast([P, P]),
                                             rows[:], start=(i == 0), stop=(i == 1))
                    last.then_inc(keys_ready, 1)

                turn(0, 0, 0)
                turn(0, 0, 1)
                keys(0, 0, 0, True)
                keys(0, 0, 1, True)

                def body(j, b, ahead, tail):
                    n = at(j, b)
                    pe.wait_ge(turned_copied, n(2, 2))
                    for c in range(G):
                        pe.wait_ge(table_ready, n(G, c + 1))
                        pe.matmul(ps[0:NB, 6, 0:P], hot_hi[:, b, c, :], hot_lo[:, b, c, :],
                                  start=False, stop=False, skip_group_check=True).then_inc(table_moved, 1)
                        pe.wait_ge(row_used[c % 2], n(4, c // 2))
                        pe.matmul(ps[:, 2 + c % 2, 0:P], hot_hi_t[:, b, c, :], table[:, c % 2, :],
                                  start=True, stop=True).then_inc(looked_up, 1)
                        if ahead and c in (3, 4):
                            turn(*ahead, c - 3)
                        if ahead and c in (5, 6):
                            keys(*ahead, c - 5)
                steps(pe, body)

        head_in = ph.sem("head_in")
        cont_step = ph.sem("cont_step")
        cont_rows = ph.sem("cont_rows")
        with ph.block() as block:
            seg_word = O.rec[0:EP].rearrange("(t q) w -> q t w", q=P)[:, :, A + SEG]

            @block.sync
            def _(sp):
                with nc.allow_non_contiguous_dma(reason="one word per tile"):
                    for t0, tile, q, lag in ((0, seg_head, 0, 0), (0, seg_prev, P - 1, 1)):
                        for k in range(TB):
                            first, last = max(k * P - lag, 0), min((k + 1) * P, T) - lag
                            p0 = lag if k == 0 else 0
                            sp.dma_start(tile[p0:p0 + last - first, k:k + 1],
                                         seg_word[q, first:last].rearrange("(t o) -> t o", o=1)).then_inc(head_in, 16)

            @block.vector
            def _(dve):
                dve.wait_ge(head_in, 16 * 2 * TB)
                dve.tensor_tensor(seg_prev[:], seg_prev[:], seg_head[:], ALU.is_equal).then_inc(cont_step, 1)
                dve.wait_ge(cont_step, 1)
                dve.tensor_tensor(O.cont_key[:], seg_prev[:], seg_head[:], ALU.mult).then_inc(cont_step, 1)
                dve.wait_ge(cont_rows, 1)
                dve.tensor_copy(O.cont_row[:, 0:512], ps[0:16, 0, :]).then_inc(cont_step, 1)
                dve.tensor_copy(O.cont_row[:, 512:TB * P], ps[0:16, 1, 0:TB * P - 512]).then_inc(cont_step, 1)
                dve.memset(O.cont_pen[:], -BIG).then_inc(cont_step, 1)
                dve.wait_ge(cont_step, 5)
                dve.tensor_tensor(O.cont_pen[:, 1:TB * P], O.cont_row[:, 1:TB * P], O.cont_row[:, 0:TB * P - 1],
                                  ALU.not_equal).then_inc(cont_step, 1)
                dve.wait_ge(cont_step, 6)
                dve.tensor_scalar(O.cont_pen[:, 1:TB * P], O.cont_pen[:, 1:TB * P], -BIG, None, ALU.mult)

            @block.tensor
            def _(pe):
                pe.wait_ge(cont_step, 2)
                for k in range(TB):
                    last = pe.matmul(ps[0:16, k // 4, P * (k % 4):P * (k % 4) + P],
                                     O.cont_key[:, k:k + 1].to_broadcast([P, 16]), C.ident[:], start=True, stop=True)
                last.then_inc(cont_rows, 1)


def spread(nc, C, O, label, table):
    with phase(nc, label) as ph:
        rows = ph.sbuf("rows", [P, NB, SPREAD_W])
        head_key = ph.sbuf("head_key", [P, TB], I32)
        heads = ph.sbuf("heads", [P, TB, SPREAD_W])
        head_at = ph.sbuf("head_at", [P, TB], I32)
        tile_i = ph.sbuf("tile_i", [P, TB], I32)
        behind = ph.sbuf("behind", [P, 1])
        home = ph.sbuf("home", [P, 3, NB])
        home_at = ph.sbuf("home_at", [P, NB], I32)
        cleared = ph.sem("cleared")
        rows_in = ph.sem("rows_in")
        keys_in = ph.sem("keys_in")
        tiles_set = ph.sem("tiles_set")
        home_step = ph.sem("home_step")
        heads_in = ph.sem("heads_in")
        homes_out = ph.sem("homes_out")
        heads_out = ph.sem("heads_out")
        unit = O.width // SPREAD_W
        word0 = (O.attrs + SPREAD) // SPREAD_W
        by_unit = O.rec.rearrange("r (u w) -> (r u) w", w=SPREAD_W)
        with ph.block() as block:
            @block.sync
            def _(sp):
                sp.dma_start(rows[:], table.rearrange("(b p) w -> p b w", p=P)).then_inc(rows_in, 16)
                sp.wait_ge(cleared, 1)
                key_word = O.rec[0:EP].rearrange("(t q) w -> q t w", q=P)[0, :, O.attrs + KEY].bitcast(I32)
                with nc.allow_non_contiguous_dma(reason="one word per tile"):
                    for k in range(TB):
                        n = min(P, T - k * P)
                        sp.dma_start(head_key[0:n, k:k + 1], key_word[k * P:k * P + n].rearrange("(t o) -> t o", o=1)
                                     ).then_inc(keys_in, 16)

            @block.vector
            def _(dve):
                dve.wait_ge(tiles_set, 1)
                dve.tensor_scalar(head_at[:], tile_i[:], float(P * unit), float(word0), ALU.mult, ALU.add)
                dve.tensor_scalar(behind[:], tile_i[:, 0:1], float(EP), None, ALU.add).then_inc(home_step, 1)
                dve.wait_ge(home_step, 1)
                dve.tensor_scalar(home[:, 0, :], O.home_i[:], behind[:], None, ALU.subtract).then_inc(home_step, 1)
                dve.wait_ge(home_step, 2)
                dve.tensor_tensor(home[:, 1, :], home[:, 0, :], O.has_edges[:], ALU.mult).then_inc(home_step, 1)
                dve.wait_ge(home_step, 3)
                dve.tensor_scalar(home[:, 2, :], home[:, 1, :], behind[:], None, ALU.add).then_inc(home_step, 1)
                dve.wait_ge(home_step, 4)
                dve.tensor_scalar(home_at[:], home[:, 2, :], float(unit), float(word0), ALU.mult, ALU.add).then_inc(home_step, 1)

            @block.gpsimd
            def _(pool):
                pool.memset(head_key[:], 0).then_inc(cleared, 1)
                pool.iota(tile_i[:], pattern=[[P, TB]], base=0, channel_multiplier=1).then_inc(tiles_set, 1)
                pool.wait_ge(keys_in, 16 * TB)
                for k in range(TB):
                    pool.indirect_dma_start(heads[:, k, :], None, table,
                                            bass.IndirectOffsetOnAxis(ap=head_key[:, k:k + 1], axis=0)).then_inc(heads_in, 16)
                pool.wait_ge(rows_in, 16)
                pool.wait_ge(home_step, 5)
                for b in range(NB):
                    pool.indirect_dma_start(by_unit, bass.IndirectOffsetOnAxis(ap=home_at[:, b:b + 1], axis=0),
                                            rows[:, b, :], None).then_inc(homes_out, 16)
                pool.wait_ge(heads_in, 16 * TB)
                pool.wait_ge(homes_out, 16 * NB)
                for k in range(TB):
                    pool.indirect_dma_start(by_unit, bass.IndirectOffsetOnAxis(ap=head_at[:, k:k + 1], axis=0),
                                            heads[:, k, :], None).then_inc(heads_out, 16)
                pool.wait_ge(heads_out, 16 * TB)


class Consts:
    pass


def make_constants(nc, ctx):
    def sb(name, shape, dt=F32):
        return ctx.enter_context(nc.sbuf_tensor(name, shape, dt))

    C = Consts()
    C.psum = ctx.enter_context(nc.psum_tensor("banks", [P, 8, 512], F32))
    C.ident, C.ident_b = sb("ident", [P, P]), sb("ident_b", [P, P], BF16)
    C.lower, C.upper = sb("lower", [P, P]), sb("upper", [P, P])
    C.ones, C.zeros = sb("ones", [P, P]), sb("zeros", [P, P])
    C.zeros_b = sb("zeros_b", [P, P], BF16)
    C.iota, C.iota_i, C.iota_b = sb("iota", [P, P]), sb("iota_i", [P, P], I32), sb("iota_b", [P, P], BF16)
    return C


def make_order(nc, ctx, label, attrs, width):
    def sb(name, shape, dt=F32):
        return ctx.enter_context(nc.sbuf_tensor(f"{label}_{name}", shape, dt))

    O = Order(attrs, width)
    O.rec = nc.dram_tensor(f"{label}_records", (TB * P * P, width), F32, kind="Internal").ap()
    O.home_i, O.has_edges = sb("home", [P, NB], I32), sb("has_edges", [P, NB])
    O.cont_key, O.cont_row, O.cont_pen = sb("cont_key", [P, TB]), sb("cont_row", [16, TB * P]), sb("cont_pen", [16, TB * P + 1])
    return O


def edge_layer(nc, C, L, label, tabs, weights):
    kind, H, O, koff = L.kind, L.heads, L.order, L.koff
    W, MW, ps = O.width, L.msg_width, C.psum
    attr_layer = kind in (0, 1)
    word0 = 0 if attr_layer else O.attrs
    RW = W - word0
    seg, key, idx = (O.attrs - word0 + w for w in (SEG, KEY, IDX_REL if kind == 2 else IDX))
    K = O.attrs + 1
    KW = {0: DIM, 1: DIM // L.heads if H else 0}.get(kind, 0)
    HG = G * H
    dh = DIM // H if H else 0
    gathers = 2 if attr_layer else 1
    bufs = BUFS[kind]
    with phase(nc, label) as ph:
        rec = ph.sbuf("rec", [P, bufs, G, RW])
        reci = rec[:].bitcast(I32)
        kv = ph.sbuf("kv", [P, bufs, G, koff + MW])
        q = ph.sbuf("q", [P, bufs, G, L.q_width]) if L.q_width else None
        same = ph.sbuf("same", [P, bufs, G, P])
        outs = ph.sbuf("outs", [P, bufs, G, L.out_width])
        if attr_layer:
            w_attr = ph.sbuf("w_attr", [K, KW])
            attr_t = ph.sbuf("attr_t", [K, G, P])
            attr_sum = ph.sbuf("attr_sum", [P, G, KW])
            prod = ph.sbuf("prod", [P, G, L.q_width])
        if H:
            score = ph.sbuf("score", [P, G, H])
            seg_wide = ph.sbuf("seg_wide", [P, G, H])
            score_raw = ph.sbuf("score_raw", [P, G, H])
            seg_t = ph.sbuf("seg_t", [HG, P])
            pen = ph.sbuf("pen", [HG, P + 1])
            run_max = ph.sbuf("run_max", [HG, P])
            seg_max = ph.sbuf("seg_max", [HG, P])
            below = ph.sbuf("below", [HG, P])
            expo = ph.sbuf("expo", [HG, P])

        weights_in = ph.sem("weights_in")
        pen_set = ph.sem("pen_set")
        rec_in = [ph.sem(f"rec_in{b}") for b in range(bufs)]
        gathered = [[ph.sem(f"gathered{b}{h}") for h in range(2)] for b in range(bufs)]
        gathers_begun = ph.sem("gathers_begun")
        same_keys = ph.sem("same_keys")
        same_done = [ph.sem(f"same_done{h}") for h in range(2)]
        msg_done = ph.sem("msg_done")
        summed = [ph.sem(f"summed{b}") for b in range(bufs)]
        out_free = [ph.sem(f"out_free{b}") for b in range(2)]
        out_copied = ph.sem("out_copied")
        stored = [ph.sem(f"stored{b}") for b in range(bufs)]
        dve_step = ph.sem("dve_step")
        act_step = ph.sem("act_step")
        if attr_layer:
            attr_turned = ph.sem("attr_turned")
            attr_copied = ph.sem("attr_copied")
            attr_mult = ph.sem("attr_mult")
            attr_moved = ph.sem("attr_moved")
            attr_begun = ph.sem("attr_begun")
        if kind == 3:
            right_ready = ph.sem("right_ready")
        if H:
            seg_wide_done = ph.sem("seg_wide_done")
            seg_turned = ph.sem("seg_turned")
            seg_copied = ph.sem("seg_copied")
            pen_done = ph.sem("pen_done")
            score_done = ph.sem("score_done")
            score_turned = ph.sem("score_turned")
            below_done = ph.sem("below_done")
            exp_done = ph.sem("exp_done")
            exp_turned = ph.sem("exp_turned")
            turns_begun = ph.sem("turns_begun")
            max_copied = ph.sem("max_copied")

        MULTS = {0: 4, 1: 1}.get(kind, 0)

        def at(j, b):
            return lambda k, o: j * (bufs * k) + (b * k + o)

        ROUNDS = STEPS // bufs

        def steps(eng, body):
            for j in repeated(eng, ROUNDS - 1):
                for b in range(bufs):
                    body(j, b, (j, b + 1) if b < bufs - 1 else (j + 1, 0))
            for b in range(bufs):
                body(ROUNDS - 1, b, (ROUNDS - 1, b + 1) if b < bufs - 1 else None)

        late = kind == 3

        def before(j, b):
            if b > 0:
                return j, b - 1
            return None if isinstance(j, int) and j == 0 else (j - 1, bufs - 1)

        with ph.block() as block:
            @block.sync
            def _(sp):
                if attr_layer:
                    col = 0
                    for w, bias in weights:
                        n_cols = w.shape[1]
                        sp.dma_start(w_attr[0:K - 1, col:col + n_cols], w).then_inc(weights_in, 16)
                        sp.dma_start(w_attr[K - 1:K, col:col + n_cols], bias.rearrange("(o n) -> o n", o=1)).then_inc(weights_in, 16)
                        col += n_cols
                records = O.rec[0:EP].rearrange("(t p) w -> p t w", p=P)

                def body(j, b, ahead):
                    sp.wait_ge(summed[b], j * G)
                    sp.dma_start(rec[:, b], records[:, bass.ds(j * (bufs * G) + b * G, G), word0:W]).then_inc(rec_in[b], 16)
                steps(sp, body)

            @block.gpsimd
            def _(pool):
                def body(j, b, ahead):
                    pool.wait_ge(rec_in[b], j * 16 + 16)
                    pool.sem_inc(gathers_begun, 1)
                    for c in range(G):
                        pool.indirect_dma_start(kv[:, b, c, 0:L.kv_width], None, tabs[0],
                                                bass.IndirectOffsetOnAxis(ap=reci[:, b, c, idx:idx + 1], axis=0)
                                                ).then_inc(gathered[b][c // 4], 16)
                        if gathers == 2:
                            pool.indirect_dma_start(q[:, b, c, :], None, tabs[1],
                                                    bass.IndirectOffsetOnAxis(ap=reci[:, b, c, key:key + 1], axis=0)
                                                    ).then_inc(gathered[b][c // 4], 16)
                steps(pool, body)

            @block.tensor
            def _(pe):
                if attr_layer:
                    pe.wait_ge(weights_in, 32 * len(weights))

                def front(j, b):
                    n = at(j, b)
                    pe.wait_ge(rec_in[b], j * 16 + 16)
                    for h in range(2):
                        pe.wait_ge(same_done[h], n(1, 0))
                        for c in range(4):
                            last = pe.matmul(ps[:, 3 + 2 * h, P * c:P * c + P],
                                             rec[:, b, 4 * h + c, seg:seg + 1].to_broadcast([P, P]), C.ident[:],
                                             start=True, stop=True)
                        last.then_inc(same_keys, 1)
                    if H:
                        if attr_layer:
                            pe.wait_ge(attr_copied, n(2, 0))
                        else:
                            pe.wait_ge(seg_copied, n(1, 0))
                        pe.wait_ge(seg_wide_done, n(1, 1))
                        pe.matmul(ps[0:HG, 0, 0:P], seg_wide[:].rearrange("p g h -> p (g h)"), C.ident[:],
                                  start=True, stop=True).then_inc(seg_turned, 1)
                    for h in range(2 if attr_layer else 0):
                        if h == 0:
                            pe.wait_ge(seg_copied, n(1, 1))
                        else:
                            pe.wait_ge(attr_copied, n(2, 1))
                        for c in range(4):
                            last = pe.transpose(ps[0:K, 0, P * c:P * c + P], rec[:, b, 4 * h + c, 0:K], C.ident[:])
                        last.then_inc(attr_turned, 1)

                def products(j, b, m, first=False):
                    n = at(j, b)
                    if kind == 0:
                        pe.wait_ge(attr_copied, n(2, m // 2 + 1))
                        if m > 1 or not first:
                            pe.wait_ge(attr_moved, n(4, m) - 1)
                        for c in range(2):
                            last = pe.matmul(ps[:, 1 + m % 2, KW * c:KW * c + KW], attr_t[:, 2 * m + c, :],
                                             w_attr[:], start=True, stop=True)
                        last.then_inc(attr_mult, 1)
                    elif kind == 1 and m == 0:
                        pe.wait_ge(attr_copied, n(2, 2))
                        pe.wait_ge(attr_moved, n(1, 0))
                        for c in range(G):
                            last = pe.matmul(ps[:, 1, KW * c:KW * c + KW], attr_t[:, c, :], w_attr[:], start=True, stop=True)
                        last.then_inc(attr_mult, 1)

                def at_edges(j, b):
                    for h in range(2):
                        pe.wait_ge(same_done[h], at(j, b)(1, 1))
                        for c in range(4 * h, 4 * h + 4):
                            last = pe.matmul(ps[:, 1, H * c:H * c + H], same[:, b, c, :], rec[:, b, c, SPREAD:SPREAD + H],
                                             start=True, stop=True)
                    last.then_inc(right_ready, 1)

                front(0, 0)
                for m in range(MULTS):
                    products(0, 0, m, True)
                if kind == 3:
                    at_edges(0, 0)

                def sums(j, b):
                    n = at(j, b)
                    for c in range(G):
                        if c % 4 == 0:
                            if H:
                                pe.wait_ge(msg_done, n(2, c // 4 + 1))
                            else:
                                pe.wait_ge(gathered[b][c // 4], j * (64 * gathers) + 64 * gathers)
                                pe.wait_ge(same_done[c // 4], n(1, 1))
                        pe.wait_ge(out_free[c % 2], n(4, c // 2))
                        pe.matmul(ps[:, 6 + c % 2, 0:MW], same[:, b, c, :], kv[:, b, c, koff:koff + MW],
                                  start=True, stop=True).then_inc(summed[b], 1)

                def body(j, b, ahead):
                    n = at(j, b)
                    if ahead:
                        front(*ahead)
                    if H:
                        pe.wait_ge(max_copied, n(1, 0))
                        pe.wait_ge(score_done, n(1, 1))
                        pe.sem_inc(turns_begun, 1)
                        pe.transpose(ps[0:HG, 4, P:2 * P], score[:].rearrange("p g h -> p (g h)"), C.ident[:]).then_inc(score_turned, 1)
                        if ahead and MULTS:
                            products(*ahead, 0)
                        pe.wait_ge(exp_done, n(1, 1))
                        pe.sem_inc(turns_begun, 1)
                        pe.transpose(ps[:, 4, 2 * P:2 * P + HG], expo[:], C.ident[0:HG, 0:HG])
                        pe.transpose(ps[:, 4, 3 * P:3 * P + HG], seg_max[:], C.ident[0:HG, 0:HG]).then_inc(exp_turned, 1)
                        for m in range(1, MULTS if ahead else 0):
                            products(*ahead, m)
                    if not late:
                        sums(j, b)
                        return
                    if before(j, b):
                        sums(*before(j, b))
                    if ahead:
                        at_edges(*ahead)
                    else:
                        sums(j, b)
                steps(pe, body)

            @block.vector
            def _(dve):
                if H:
                    dve.memset(pen[:], -BIG).then_inc(pen_set, 1)
                    dve.wait_ge(pen_set, 1)
                links = {0: 4, 1: 5, 3: 3}.get(kind, 0)

                def wide(j, b):
                    dve.wait_ge(rec_in[b], j * 16 + 16)
                    dve.tensor_copy(seg_wide[:], rec[:, b, :, seg:seg + 1].to_broadcast([P, G, H])).then_inc(seg_wide_done, 1)

                def make_same(j, b, h):
                    dve.wait_ge(summed[b], j * G)
                    dve.wait_ge(same_keys, at(j, b)(2, h + 1))
                    dve.tensor_tensor(same[:, b, 4 * h:4 * h + 4, :], ps[:, 3 + 2 * h, :].rearrange("p (c e) -> p c e", c=4),
                                      rec[:, b, 4 * h:4 * h + 4, seg:seg + 1].to_broadcast([P, 4, P]),
                                      ALU.is_equal).then_inc(same_done[h], 1)

                def penalties(j, b):
                    dve.wait_ge(seg_copied, at(j, b)(1, 1))
                    dve.tensor_tensor(pen[:, 1:P], seg_t[:, 0:P - 1], seg_t[:, 1:P], ALU.subtract).then_inc(pen_done, 1)

                if H:
                    wide(0, 0)
                make_same(0, 0, 0)
                make_same(0, 0, 1)
                if H:
                    penalties(0, 0)

                def body(j, b, ahead):
                    n = at(j, b)
                    made = [0]

                    def link(ins):
                        made[0] += 1
                        ins.then_inc(dve_step, 1)
                        dve.wait_ge(dve_step, n(links, made[0]))

                    if not H:
                        if ahead:
                            make_same(*ahead, 0)
                            make_same(*ahead, 1)
                        return
                    if ahead:
                        wide(*ahead)
                    for h in range(2):
                        t = slice(4 * h, 4 * h + 4)
                        dve.wait_ge(gathered[b][h], j * (64 * gathers) + 64 * gathers)
                        if kind == 0:
                            dve.wait_ge(attr_moved, n(4, 2 * h + 2))
                            dve.tensor_tensor(kv[:, b, t, 0:P], attr_sum[:, t, 0:P], kv[:, b, t, 0:P], ALU.add)
                            last = dve.tensor_tensor(q[:, b, t, :], attr_sum[:, t, P:2 * P], q[:, b, t, :], ALU.add)
                        if kind == 1:
                            dve.wait_ge(attr_moved, n(1, 1))
                            k4 = kv[:, b, t, 0:DIM].rearrange("p c (h d) -> p c h d", h=H)
                            last = dve.tensor_tensor(k4, attr_sum[:, t, :].unsqueeze(2).to_broadcast([P, 4, H, KW]), k4, ALU.add)
                    if attr_layer:
                        link(last)
                        link(dve.tensor_tensor(prod[:], kv[:, b, :, 0:L.q_width], q[:, b], ALU.mult))
                        to = score_raw if kind == 1 else score
                        ins = dve.tensor_reduce(to[:], prod[:].rearrange("p g (h d) -> p g h d", h=H), AX_X, ALU.add)
                        if kind == 0:
                            ins.then_inc(score_done, 1)
                        else:
                            link(ins)
                            wt = rec[:, b, :, O.attrs + WEIGHT:O.attrs + WEIGHT + 1].to_broadcast([P, G, H])
                            dve.tensor_tensor(score[:], score_raw[:], wt, ALU.mult).then_inc(score_done, 1)
                    if kind == 3:
                        dve.wait_ge(right_ready, n(1, 1))
                        link(dve.tensor_tensor(score_raw[:], kv[:, b, :, 0:H],
                                               ps[:, 1, 0:HG].rearrange("p (g h) -> p g h", g=G), ALU.add))
                        dve.scalar_tensor_tensor(out=score[:], in0=score_raw[:], scalar=0.2, in1=score_raw[:],
                                                 op0=ALU.mult, op1=ALU.max).then_inc(score_done, 1)
                    if ahead:
                        make_same(*ahead, 0)
                    dve.wait_ge(score_turned, n(1, 1))
                    dve.wait_ge(pen_done, n(1, 1))
                    sc_t = ps[0:HG, 4, P:2 * P]
                    link(dve.tensor_tensor_scan(run_max[:], pen[:, 0:P], sc_t, -BIG, ALU.add, ALU.max))
                    link(dve.tensor_tensor_scan(seg_max[:, ::-1], pen[:, 1:P + 1][:, ::-1], run_max[:, ::-1], -BIG,
                                                ALU.add, ALU.max))
                    dve.tensor_tensor(below[:], sc_t, seg_max[:], ALU.subtract).then_inc(below_done, 1)
                    if ahead:
                        make_same(*ahead, 1)
                        penalties(*ahead)
                    dve.wait_ge(exp_turned, n(1, 1))
                    for h in range(2):
                        t = slice(4 * h, 4 * h + 4)
                        v4 = kv[:, b, t, koff:koff + DIM].rearrange("p c (h d) -> p c h d", h=H)
                        e3 = ps[:, 4, 2 * P + 4 * H * h:2 * P + 4 * H * h + 4 * H].rearrange("p (c h) -> p c h", c=4)
                        dve.tensor_copy(kv[:, b, t, koff + DIM:koff + DIM + H], e3)
                        dve.tensor_tensor(v4, v4, bc(e3, dh), ALU.mult).then_inc(msg_done, 1)
                    assert made[0] == links
                steps(dve, body)

            @block.scalar
            def _(act):
                rows = C.sums[:, 0:L.out_width].rearrange("(t p) w -> p t w", p=P)

                def front(j, b):
                    n = at(j, b)
                    if H:
                        act.wait_ge(seg_turned, n(1, 1))
                        act.wait_ge(pen_done, n(1, 0))
                        act.mul(seg_t[:], ps[0:HG, 0, 0:P], BIG).then_inc(seg_copied, 1)
                    for h in range(2 if attr_layer else 0):
                        act.wait_ge(attr_turned, n(2, h + 1))
                        act.wait_ge(attr_mult, n(MULTS, 0))
                        act.copy(attr_t[:, 4 * h:4 * h + 4, :], ps[0:K, 0, :].rearrange("k (c e) -> k c e", c=4)).then_inc(attr_copied, 1)

                def move_products(j, b):
                    per = G // MULTS
                    for m in range(MULTS):
                        act.wait_ge(attr_mult, at(j, b)(MULTS, m + 1))
                        act.copy(attr_sum[:, m * per:m * per + per, :],
                                 ps[:, 1 + m % 2, 0:per * KW].rearrange("p (c w) -> p c w", c=per)).then_inc(attr_moved, 1)

                def move_sums(j, b, c0, c1):
                    for c in range(c0, c1):
                        act.wait_ge(summed[b], j * G + c + 1)
                        act.copy(outs[:, b, c, 0:MW], ps[:, 6 + c % 2, 0:MW]).then_inc(out_free[c % 2], 1)

                def store(j, b):
                    for h in range(2):
                        act.wait_ge(out_free[h], at(j, b)(4, 4))
                    if H:
                        act.wait_ge(max_copied, at(j, b)(1, 1))
                    act.dma_start(rows[:, bass.ds(j * (bufs * G) + b * G, G), :], outs[:, b]).then_inc(stored[b], 16)

                front(0, 0)
                if MULTS:
                    move_products(0, 0)

                def body(j, b, ahead):
                    n = at(j, b)
                    if ahead and H:
                        front(*ahead)
                    if H:
                        act.wait_ge(below_done, n(1, 1))
                        act.activation(expo[:], below[:], ACT.Exp).then_inc(exp_done, 1)
                    if ahead and MULTS:
                        move_products(*ahead)
                    act.wait_ge(stored[b], j * 16)
                    if late and before(j, b):
                        move_sums(*before(j, b), 0, G // 2)
                    if H:
                        act.wait_ge(msg_done, n(2, 2))
                        act.copy(outs[:, b, :, MW:MW + H], ps[:, 4, 3 * P:3 * P + HG].rearrange("p (g h) -> p g h", g=G)).then_inc(max_copied, 1)
                    if late and before(j, b):
                        move_sums(*before(j, b), G // 2, G)
                        store(*before(j, b))
                    if not late or not ahead:
                        move_sums(j, b, 0, G)
                        store(j, b)
                steps(act, body)
                for b in range(bufs):
                    act.wait_ge(stored[b], ROUNDS * 16)


def combine(nc, C, L, label, target, add):
    H, O, MW, OW, ps = L.heads, L.order, L.msg_width, L.out_width, C.psum
    CW = OW + (1 if H else 0)
    CNT = OW
    dh = DIM // H if H else 0
    with phase(nc, label) as ph:
        conts = ph.sbuf("conts", [P, TB, CW])
        left = ph.sbuf("left", [P, TB, CW])
        parts = ph.sbuf("parts", [P, 3, TB, CW], BF16)
        pick = ph.sbuf("pick", [P, 2, TB, P], BF16)
        node_id = ph.sbuf("node_id", [P, 2, P])
        home = ph.sbuf("home", [P, NB, OW])
        more = ph.sbuf("more", [P, NB, CW])
        if H:
            max_row = ph.sbuf("max_row", [H, TB * P])
            run_max = ph.sbuf("run_max", [H, TB * P])
            factor = ph.sbuf("factor", [P, TB, H])
            below = ph.sbuf("below", [P, TB, H])
            count = ph.sbuf("count", [P, 3, NB])
            shift = ph.sbuf("shift", [P, 2, NB, H])
            most = ph.sbuf("most", [P, NB, H])
            scale = ph.sbuf("scale", [P, 2, NB, H])

        cleared = ph.sem("cleared")
        conts_in = ph.sem("conts_in")
        max_turned = ph.sem("max_turned")
        row_ready = ph.sem("row_ready")
        conts_scaled = ph.sem("conts_scaled")
        exp_done = ph.sem("exp_done")
        dve_step = ph.sem("dve_step")
        home_in = ph.sem("home_in")
        with ph.block() as block:
            first_rows = C.sums[:, 0:OW].rearrange("(t q) w -> q t w", q=P)[0]

            @block.gpsimd
            def _(pool):
                pool.memset(conts[:, TB - 1, :], 0.0).then_inc(cleared, 1)
                for b in range(NB):
                    pool.indirect_dma_start(home[:, b, :], None, C.sums,
                                            bass.IndirectOffsetOnAxis(ap=O.home_i[:, b:b + 1], axis=0)).then_inc(home_in, 16)

            @block.sync
            def _(sp):
                sp.wait_ge(cleared, 1)
                sp.dma_start(conts[:, 0:TB - 1, 0:OW],
                             first_rows[0:(TB - 1) * P].rearrange("(b p) w -> p b w", p=P)).then_inc(conts_in, 16)
                sp.dma_start(conts[0:TLAST, TB - 1, 0:OW], first_rows[(TB - 1) * P:T]).then_inc(conts_in, 16)

            if H:
                @block.tensor
                def _(pe):
                    pe.wait_ge(conts_in, 32)
                    for k in range(TB):
                        last = pe.transpose(ps[0:H, k // 4, P * (k % 4):P * (k % 4) + P], conts[:, k, MW:MW + H], C.ident[:])
                    last.then_inc(max_turned, 1)
                    pe.wait_ge(row_ready, 1)
                    for k in range(TB):
                        last = pe.transpose(ps[:, 2, H * k:H * k + H], max_row[:, P * k:P * k + P], C.ident[0:H, 0:H])
                    last.then_inc(max_turned, 1)

                @block.scalar
                def _(act):
                    act.wait_ge(conts_scaled, 1)
                    act.activation(factor[:], below[:], ACT.Exp).then_inc(exp_done, 1)

            @block.vector
            def _(dve):
                made = [0]

                def link(ins):
                    made[0] += 1
                    ins.then_inc(dve_step, 1)
                    dve.wait_ge(dve_step, made[0])

                for h in range(2):
                    dve.tensor_scalar(node_id[:, h, :], C.iota[:], 1.0 + P * h, None, ALU.add)
                if H:
                    dve.wait_ge(max_turned, 1)
                    dve.tensor_copy(max_row[:, 0:512], ps[0:H, 0, :])
                    link(dve.tensor_copy(max_row[:, 512:TB * P], ps[0:H, 1, 0:TB * P - 512]))
                    link(dve.tensor_tensor_scan(run_max[:], O.cont_pen[0:H, 0:TB * P], max_row[:], -BIG, ALU.add, ALU.max))
                    dve.tensor_tensor_scan(max_row[:, ::-1], O.cont_pen[0:H, 1:TB * P + 1][:, ::-1], run_max[:, ::-1], -BIG,
                                           ALU.add, ALU.max).then_inc(row_ready, 1)
                    dve.wait_ge(max_turned, 2)
                    turned = ps[:, 2, 0:TB * H].rearrange("p (k h) -> p k h", k=TB)
                    dve.tensor_tensor(below[:], conts[:, :, MW:MW + H], turned, ALU.subtract).then_inc(conts_scaled, 1)
                    dve.wait_ge(conts_scaled, 1)
                    link(dve.tensor_copy(conts[:, :, MW:MW + H], turned))
                    dve.memset(conts[:, :, CNT:CNT + 1], 1.0)
                    dve.wait_ge(exp_done, 1)
                    v = conts[:, :, 0:DIM].rearrange("p k (h d) -> p k h d", h=H)
                    dve.tensor_tensor(v, v, bc(factor[:], dh), ALU.mult)
                    link(dve.tensor_tensor(conts[:, :, DIM:MW], conts[:, :, DIM:MW], factor[:], ALU.mult))
                else:
                    dve.wait_ge(conts_in, 32)
                link(dve.tensor_copy(parts[:, 0], conts[:]))
                link(dve.tensor_tensor(left[:], conts[:], parts[:, 0], ALU.subtract))
                link(dve.tensor_copy(parts[:, 1], left[:]))
                link(dve.tensor_tensor(conts[:], left[:], parts[:, 1], ALU.subtract))
                link(dve.tensor_copy(parts[:, 2], conts[:]))

        pick_ready = [ph.sem(f"pick_ready{h}") for h in range(2)]
        ids_moved = ph.sem("ids_moved")
        conts_summed = [ph.sem(f"conts_summed{h}") for h in range(2)]
        more_copied = [ph.sem(f"more_copied{h}") for h in range(2)]
        copies_begun = ph.sem("copies_begun")

        def blocks(eng, body):
            for j in repeated(eng, NB // 2):
                body(j, 0)
                body(j, 1)
            for h in range(NB % 2):
                body(NB // 2, h)

        with ph.block() as block:
            @block.vector
            def _(dve):
                def body(j, h):
                    dve.wait_ge(conts_summed[h], j)
                    dve.tensor_tensor(pick[:, h], node_id[:, h, :].unsqueeze(1).to_broadcast([P, TB, P]),
                                      bc(O.cont_key[:], P), ALU.is_equal).then_inc(pick_ready[h], 1)
                    dve.wait_ge(pick_ready[h], j + 1)
                    dve.tensor_scalar(node_id[:, h, :], node_id[:, h, :], 2.0 * P, None, ALU.add).then_inc(ids_moved, 1)
                    dve.wait_ge(ids_moved, j * 2 + h + 1)
                blocks(dve, body)

            @block.tensor
            def _(pe):
                def body(j, h):
                    pe.wait_ge(pick_ready[h], j + 1)
                    pe.wait_ge(more_copied[h], j)
                    for k in range(TB):
                        for i in range(3):
                            last = pe.matmul(ps[:, 3 + h, 0:CW], pick[:, h, k, :], parts[:, i, k, :],
                                             start=(k == 0 and i == 0), stop=(k == TB - 1 and i == 2))
                    last.then_inc(conts_summed[h], 1)
                blocks(pe, body)

            @block.scalar
            def _(act):
                def body(j, h):
                    act.wait_ge(conts_summed[h], j + 1)
                    act.sem_inc(copies_begun, 1)
                    act.copy(more[:, bass.ds(j * 2 + h, 1), :].rearrange("p o w -> p (o w)"), ps[:, 3 + h, 0:CW]
                             ).then_inc(more_copied[h], 1)
                blocks(act, body)

        shift_ready = ph.sem("shift_ready")
        scale_ready = ph.sem("scale_ready")
        order_step = ph.sem("order_step")
        with ph.block() as block:
            if H:
                @block.scalar
                def _(act):
                    act.wait_ge(shift_ready, 1)
                    act.activation(scale[:], shift[:], ACT.Exp).then_inc(scale_ready, 1)

            @block.vector
            def _(dve):
                made = [0]

                def link(ins):
                    made[0] += 1
                    ins.then_inc(order_step, 1)
                    dve.wait_ge(order_step, made[0])

                has = O.has_edges[:]
                dve.wait_ge(home_in, 16 * NB)
                if not H:
                    link(dve.tensor_tensor(home[:], home[:], bc(has, DIM), ALU.mult))
                    dve.tensor_tensor(target[:], home[:], more[:], ALU.add)
                    return
                n_conts = more[:, :, CNT]
                dve.tensor_scalar(count[:, 0, :], n_conts, 0.0, -BIG, ALU.is_equal, ALU.mult)
                link(dve.tensor_scalar(count[:, 1, :], n_conts, 1.0, None, ALU.max))
                link(dve.reciprocal(count[:, 2, :], count[:, 1, :]))
                link(dve.tensor_tensor(shift[:, 0], more[:, :, MW:MW + H], bc(count[:, 2, :], H), ALU.mult))
                link(dve.tensor_tensor(shift[:, 1], shift[:, 0], bc(count[:, 0, :], H), ALU.add))
                link(dve.tensor_tensor(most[:], shift[:, 1], home[:, :, MW:MW + H], ALU.max))
                dve.tensor_tensor(shift[:, 0], home[:, :, MW:MW + H], most[:], ALU.subtract)
                dve.tensor_tensor(shift[:, 1], shift[:, 1], most[:], ALU.subtract).then_inc(shift_ready, 1)
                dve.wait_ge(scale_ready, 1)
                heads = lambda t: t[:, :, 0:DIM].rearrange("p b (h d) -> p b h d", h=H)
                for s, rows in enumerate((home, more)):
                    dve.tensor_tensor(heads(rows), heads(rows), bc(scale[:, s], dh), ALU.mult)
                    last = dve.tensor_tensor(rows[:, :, DIM:MW], rows[:, :, DIM:MW], scale[:, s], ALU.mult)
                link(last)
                dve.tensor_tensor(home[:, :, 0:DIM], home[:, :, 0:DIM], more[:, :, 0:DIM], ALU.add)
                link(dve.scalar_tensor_tensor(out=most[:], in0=home[:, :, DIM:MW], scalar=DEN_EPS, in1=more[:, :, DIM:MW],
                                              op0=ALU.add, op1=ALU.add))
                link(dve.reciprocal(shift[:, 0], most[:]))
                link(dve.tensor_tensor(shift[:, 1], shift[:, 0], bc(has, H), ALU.mult))
                into = home if add else target
                ins = dve.tensor_tensor(heads(into), heads(home), bc(shift[:, 1], dh), ALU.mult)
                if add:
                    link(ins)
                    dve.tensor_tensor(target[:], target[:], home[:, :, 0:DIM], ALU.add)


def blocks_ahead(eng, body):
    for j in repeated(eng, NB // 2):
        body(j, 0, (j, 1))
        body(j, 1, (j + 1, 0))
    body(NB // 2, 0, None)


def layer_norm(nc, C, label, src, dst, affine=None, relu=True):
    with phase(nc, label) as ph:
        stats = ph.sbuf("stats", [P, NB, 6])
        moments = ph.sbuf("moments", [P, NB, 2])
        root = ph.sbuf("root", [P, 3, NB])
        shift = ph.sbuf("shift", [P, NB])
        if affine is not None:
            gb = ph.sbuf("gb", [P, 2, DIM])
        vectors_in = ph.sem("vectors_in")
        dve_step = ph.sem("dve_step")
        root_done = ph.sem("root_done")
        scale_ready = ph.sem("scale_ready")
        normed = ph.sem("normed")
        with ph.block() as block:
            @block.sync
            def _(sp):
                if affine is not None:
                    for i, v in enumerate(affine):
                        sp.dma_start(gb[:, i, :], v.rearrange("(o n) -> o n", o=1).to_broadcast([P, DIM])).then_inc(vectors_in, 16)

            @block.scalar
            def _(act):
                act.wait_ge(dve_step, 3)
                act.activation(root[:, 1, :], root[:, 0, :], ACT.Sqrt).then_inc(root_done, 1)
                act.wait_ge(scale_ready, 1)
                for b in range(NB):
                    act.activation(dst[:, b, :], src[:, b, :], ACT.Relu if relu else ACT.Identity,
                                   bias=shift[:, b:b + 1], scale=root[:, 2, b:b + 1]).then_inc(normed, 1)

            @block.vector
            def _(dve):
                for b in range(NB):
                    last = dve.bn_stats(out=stats[:, b, :], in_=src[:, b, :])
                last.then_inc(dve_step, 1)
                dve.wait_ge(dve_step, 1)
                for b in range(NB):
                    last = dve.bn_aggr(out=moments[:, b, :], in_=stats[:, b, :])
                last.then_inc(dve_step, 1)
                dve.wait_ge(dve_step, 2)
                dve.tensor_scalar(root[:, 0, :], moments[:, :, 1], LN_EPS, None, ALU.add).then_inc(dve_step, 1)
                dve.wait_ge(root_done, 1)
                dve.reciprocal(root[:, 2, :], root[:, 1, :]).then_inc(dve_step, 1)
                dve.wait_ge(dve_step, 4)
                dve.scalar_tensor_tensor(out=shift[:], in0=moments[:, :, 0], scalar=-1.0, in1=root[:, 2, :],
                                         op0=ALU.mult, op1=ALU.mult).then_inc(scale_ready, 1)
                if affine is None:
                    return
                dve.wait_ge(vectors_in, 32)
                done = 4
                for b0 in range(0, NB, 5):
                    part = dst[:, b0:b0 + 5, :]
                    dve.wait_ge(normed, b0 + 5)
                    for i, op in enumerate((ALU.mult, ALU.add)):
                        dve.tensor_tensor(part, part, gb[:, i, :].unsqueeze(1).to_broadcast([P, 5, DIM]), op).then_inc(dve_step, 1)
                        done += 1
                        dve.wait_ge(dve_step, done)


def project(nc, C, label, src, parts, scales, stores, scores=None):
    ps = C.psum
    total = sum(w.shape[1] for w, _ in parts)
    banks = [(c, min(c + 512, total)) for c in range(0, total, 512)]
    CH = len(banks)
    apart = CH <= 2
    biased = parts[0][1] is not None
    with phase(nc, label) as ph:
        weight = ph.sbuf("weight", [P, 2, total])
        cur = ph.sbuf("cur", [P, 2, DIM])
        cur_t = ph.sbuf("cur_t", [P, 2, 2, P])
        stage = ph.sbuf("stage", [P, 2, total])
        if biased:
            bias = ph.sbuf("bias", [P, total])
        if scores is not None:
            att = ph.sbuf("att", [P, 2, DIM])
            att_prod = ph.sbuf("att_prod", [P, 2, DIM])
            att_sum = ph.sbuf("att_sum", [P, 2, 2, scores[1]])
        weights_in = ph.sem("weights_in")
        bias_scaled = ph.sem("bias_scaled")
        cur_ready = ph.sem("cur_ready")
        turned = ph.sem("turned")
        turned_copied = ph.sem("turned_copied")
        mult_done = ph.sem("mult_done")
        staged = ph.sem("staged")
        stored = [ph.sem(f"stored{h}") for h in range(2)]
        scored = ph.sem("scored")
        stage_begun = ph.sem("stage_begun")
        stores_begun = ph.sem("stores_begun")
        evacs = len(scales)
        n_loads = len(parts) + sum(b is not None for _, b in parts) + (2 if scores is not None else 0)

        def outputs(rows, h):
            return stores(rows, stage[:, h, :], att_sum[:, h] if scores is not None else None)

        outs = len(outputs(slice(0, P), 0))

        def at(j, h):
            return lambda k, o: j * (2 * k) + (h * k + o)

        def bank(h, i):
            return 2 + (h * CH if apart else 0) + i

        with ph.block() as block:
            @block.sync
            def _(sp):
                col = 0
                for w, vec in parts:
                    cols = slice(col, col + w.shape[1])
                    sp.dma_start(weight[:, :, cols], w.rearrange("(k p) n -> p k n", p=P)).then_inc(weights_in, 16)
                    if vec is not None:
                        sp.dma_start(bias[:, cols], vec.rearrange("(o n) -> o n", o=1).to_broadcast([P, w.shape[1]])).then_inc(weights_in, 16)
                    col += w.shape[1]
                if scores is not None:
                    for i in range(2):
                        sp.dma_start(att[:, i, :], scores[0][i].rearrange("h d -> (h d)").rearrange("(o n) -> o n", o=1)
                                     .to_broadcast([P, DIM])).then_inc(weights_in, 16)

                def body(j, h, ahead):
                    n = at(j, h)
                    sp.wait_ge(staged, n(evacs, evacs))
                    if scores is not None:
                        sp.sem_inc(stores_begun, 1)
                        sp.wait_ge(scored, n(2, 2))
                    sp.sem_inc(stores_begun, 1)
                    for dst, src_ap in outputs(bass.ds(j * (2 * P) + h * P, P), h):
                        sp.dma_start(dst, src_ap).then_inc(stored[h], 16)
                blocks_ahead(sp, body)
                for h in range(2):
                    sp.wait_ge(stored[h], (NB + 1 - h) // 2 * outs * 16)

            def evacuate(eng, j, h, scale_add):
                n = at(j, h)
                eng.wait_ge(stored[h], j * (outs * 16))
                for i, (c0, c1, factor) in enumerate(scales):
                    eng.wait_ge(mult_done, n(CH, c0 // 512 + 1))
                    eng.sem_inc(stage_begun, 1)
                    scale_add(stage[:, h, c0:c1], ps[:, bank(h, c0 // 512), c0 % 512:c0 % 512 + c1 - c0], c0, c1, factor
                              ).then_inc(staged, 1)

            @block.vector
            def _(dve):
                dve.wait_ge(weights_in, 16 * n_loads)
                if biased:
                    for i, (c0, c1, factor) in enumerate(scales):
                        dve.tensor_scalar(bias[:, c0:c1], bias[:, c0:c1], factor, None, ALU.mult).then_inc(bias_scaled, 1)
                    dve.wait_ge(bias_scaled, evacs)

                def take(j, h):
                    dve.tensor_scalar(cur[:, h, :], src[:, bass.ds(j * 2 + h, 1), :].rearrange("p o w -> p (o w)"), 1.0, None,
                                      ALU.mult).then_inc(cur_ready, 1)

                take(0, 0)

                def body(j, h, ahead):
                    n = at(j, h)
                    if ahead:
                        dve.wait_ge(turned, n(1, 0))
                        take(*ahead)
                    if biased:
                        evacuate(dve, j, h, lambda out, sums, c0, c1, factor: dve.scalar_tensor_tensor(
                            out=out, in0=sums, scalar=factor, in1=bias[:, c0:c1], op0=ALU.mult, op1=ALU.add))
                    if scores is not None:
                        dve.wait_ge(staged, n(evacs, evacs))
                        dve.wait_ge(scored, n(2, 0))
                        dve.tensor_tensor(att_prod[:], stage[:, h, :].unsqueeze(1).to_broadcast([P, 2, DIM]), att[:], ALU.mult).then_inc(scored, 1)
                        dve.wait_ge(scored, n(2, 1))
                        dve.wait_ge(stored[h], j * (outs * 16))
                        dve.tensor_reduce(att_sum[:, h], att_prod[:].rearrange("p s (h d) -> p s h d", h=scores[1]), AX_X,
                                          ALU.add).then_inc(scored, 1)
                blocks_ahead(dve, body)

            @block.tensor
            def _(pe):
                pe.wait_ge(weights_in, 16 * n_loads)

                def turn(j, h):
                    pe.wait_ge(cur_ready, at(j, h)(1, 1))
                    for k in range(2):
                        last = pe.transpose(ps[:, h, P * k:P * k + P], cur[:, h, P * k:P * k + P], C.ident[:])
                    last.then_inc(turned, 1)

                turn(0, 0)

                def body(j, h, ahead):
                    n = at(j, h)
                    first = isinstance(j, int) and j == 0
                    if ahead:
                        pe.wait_ge(turned_copied, n(1, 0))
                        turn(*ahead)
                    pe.wait_ge(turned_copied, n(1, 1))
                    for i, (c0, c1) in enumerate(banks):
                        if apart and i == 0 and not first:
                            pe.wait_ge(staged, n(evacs, 0) - evacs)
                        if not apart and not (first and h == 0):
                            pe.wait_ge(staged, n(evacs, i + 1) - evacs)
                        for k in range(2):
                            last = pe.matmul(ps[:, bank(h, i), 0:c1 - c0], cur_t[:, h, k, :], weight[:, k, c0:c1],
                                             start=(k == 0), stop=(k == 1))
                        last.then_inc(mult_done, 1)
                blocks_ahead(pe, body)

            @block.scalar
            def _(act):
                def copy_turned(j, h):
                    act.wait_ge(turned, at(j, h)(1, 1))
                    act.copy(cur_t[:, h], ps[:, h, 0:2 * P].rearrange("p (k e) -> p k e", k=2)).then_inc(turned_copied, 1)

                copy_turned(0, 0)

                def body(j, h, ahead):
                    if ahead:
                        act.wait_ge(mult_done, at(j, h)(CH, 0))
                        copy_turned(*ahead)
                    if not biased:
                        evacuate(act, j, h, lambda out, sums, c0, c1, factor: act.mul(out, sums, factor))
                blocks_ahead(act, body)


def output_projection(nc, C, label, src, into, w_dram, b_dram, alpha_dram):
    ps = C.psum
    with phase(nc, label) as ph:
        weight = ph.sbuf("weight", [P, 2, DIM])
        bias = ph.sbuf("bias", [P, DIM])
        alpha = ph.sbuf("alpha", [P, 1])
        cur = ph.sbuf("cur", [P, 2, DIM])
        cur_t = ph.sbuf("cur_t", [P, 2, 2, P])
        weights_in = ph.sem("weights_in")
        bias_step = ph.sem("bias_step")
        cur_ready = ph.sem("cur_ready")
        turned = ph.sem("turned")
        turned_copied = ph.sem("turned_copied")
        mult_done = ph.sem("mult_done")
        added = ph.sem("added")

        def at(j, h):
            return lambda k, o: j * (2 * k) + (h * k + o)

        with ph.block() as block:
            @block.sync
            def _(sp):
                sp.dma_start(weight[:], w_dram.rearrange("(k p) n -> p k n", p=P)).then_inc(weights_in, 16)
                sp.dma_start(bias[:], b_dram.rearrange("(o n) -> o n", o=1).to_broadcast([P, DIM])).then_inc(weights_in, 16)
                sp.dma_start(alpha[:], alpha_dram.rearrange("(o n) -> o n", o=1).to_broadcast([P, 1])).then_inc(weights_in, 16)

            @block.vector
            def _(dve):
                def take(j, h):
                    dve.tensor_scalar(cur[:, h, :], src[:, bass.ds(j * 2 + h, 1), :].rearrange("p o w -> p (o w)"), 1.0, None,
                                      ALU.mult).then_inc(cur_ready, 1)

                take(0, 0)
                dve.wait_ge(weights_in, 48)
                dve.tensor_scalar(bias[:], bias[:], alpha[:], None, ALU.mult).then_inc(bias_step, 1)
                dve.wait_ge(bias_step, 1)
                dve.tensor_tensor(into[:], into[:], bias[:].unsqueeze(1).to_broadcast([P, NB, DIM]), ALU.add).then_inc(bias_step, 1)
                dve.wait_ge(bias_step, 2)

                def body(j, h, ahead):
                    if ahead:
                        dve.wait_ge(turned, at(j, h)(1, 0))
                        take(*ahead)
                    dve.wait_ge(mult_done, at(j, h)(1, 1))
                    y = into[:, bass.ds(j * 2 + h, 1), :].rearrange("p o w -> p (o w)")
                    dve.scalar_tensor_tensor(out=y, in0=ps[:, 2 + h, 0:DIM], scalar=alpha[:], in1=y, op0=ALU.mult,
                                             op1=ALU.add).then_inc(added, 1)
                blocks_ahead(dve, body)

            @block.tensor
            def _(pe):
                pe.wait_ge(weights_in, 48)

                def turn(j, h):
                    pe.wait_ge(cur_ready, at(j, h)(1, 1))
                    for k in range(2):
                        last = pe.transpose(ps[:, h, P * k:P * k + P], cur[:, h, P * k:P * k + P], C.ident[:])
                    last.then_inc(turned, 1)

                turn(0, 0)

                def body(j, h, ahead):
                    n = at(j, h)
                    if ahead:
                        pe.wait_ge(turned_copied, n(1, 0))
                        turn(*ahead)
                    pe.wait_ge(turned_copied, n(1, 1))
                    if not (isinstance(j, int) and j == 0):
                        pe.wait_ge(added, n(1, 0) - 1)
                    for k in range(2):
                        last = pe.matmul(ps[:, 2 + h, 0:DIM], cur_t[:, h, k, :], weight[:, k, :], start=(k == 0), stop=(k == 1))
                    last.then_inc(mult_done, 1)
                blocks_ahead(pe, body)

            @block.scalar
            def _(act):
                def copy_turned(j, h):
                    act.wait_ge(turned, at(j, h)(1, 1))
                    act.copy(cur_t[:, h], ps[:, h, 0:2 * P].rearrange("p (k e) -> p k e", k=2)).then_inc(turned_copied, 1)

                copy_turned(0, 0)

                def body(j, h, ahead):
                    if ahead:
                        act.wait_ge(mult_done, at(j, h)(1, 0))
                        copy_turned(*ahead)
                blocks_ahead(act, body)


def feed_forward(nc, C, label, src, y, x, w1, b1, w2, b2, beta_dram):
    ps = C.psum
    FF = w1.shape[1]
    FB = FF // P
    with phase(nc, label) as ph:
        weight1 = ph.sbuf("weight1", [P, 2, FF])
        weight2 = ph.sbuf("weight2", [P, FB, DIM])
        bias1 = ph.sbuf("bias1", [P, FB])
        bias2 = ph.sbuf("bias2", [1, DIM])
        beta = ph.sbuf("beta", [P, 1])
        cur = ph.sbuf("cur", [P, DIM])
        cur_t = ph.sbuf("cur_t", [P, 2, P])
        hidden = ph.sbuf("hidden", [P, FB, P])
        delta = ph.sbuf("delta", [P, DIM])
        weights_in = ph.sem("weights_in")
        cur_ready = ph.sem("cur_ready")
        turned = ph.sem("turned")
        turned_copied = ph.sem("turned_copied")
        hidden_mult = ph.sem("hidden_mult")
        hidden_ready = ph.sem("hidden_ready")
        mult_done = ph.sem("mult_done")
        delta_ready = ph.sem("delta_ready")
        with ph.block() as block:
            @block.sync
            def _(sp):
                sp.dma_start(weight1[:], w1.rearrange("(k p) n -> p k n", p=P)).then_inc(weights_in, 16)
                sp.dma_start(weight2[:], w2.rearrange("(k p) n -> p k n", p=P)).then_inc(weights_in, 16)
                with nc.allow_non_contiguous_dma(reason="a bias per partition"):
                    for f in range(FB):
                        sp.dma_start(bias1[:, f:f + 1], b1[f * P:f * P + P].rearrange("(p o) -> p o", o=1)).then_inc(weights_in, 16)
                sp.dma_start(bias2[:], b2.rearrange("(o n) -> o n", o=1)).then_inc(weights_in, 16)
                sp.dma_start(beta[:], beta_dram.rearrange("(o n) -> o n", o=1).to_broadcast([P, 1])).then_inc(weights_in, 16)

            loads = 16 * (4 + FB)

            @block.vector
            def _(dve):
                dve.wait_ge(weights_in, loads)
                for b in repeated(dve, NB):
                    blk = bass.ds(b, 1)
                    flat = lambda t: t[:, blk, :].rearrange("p o w -> p (o w)")
                    dve.wait_ge(turned, b)
                    dve.tensor_scalar(cur[:], flat(src), 1.0, None, ALU.mult).then_inc(cur_ready, 1)
                    dve.tensor_tensor(flat(x), flat(x), flat(y), ALU.add).then_inc(delta_ready, 1)
                    dve.wait_ge(mult_done, b + 1)
                    dve.wait_ge(delta_ready, b * 2 + 1)
                    dve.scalar_tensor_tensor(out=flat(x), in0=ps[:, 3, 0:DIM], scalar=beta[:], in1=flat(x), op0=ALU.mult,
                                             op1=ALU.add).then_inc(delta_ready, 1)

            @block.tensor
            def _(pe):
                pe.wait_ge(weights_in, loads)
                for b in repeated(pe, NB):
                    pe.wait_ge(cur_ready, b + 1)
                    for k in range(2):
                        last = pe.transpose(ps[:, 0, P * k:P * k + P], cur[:, P * k:P * k + P], C.ident[:])
                    last.then_inc(turned, 1)
                    pe.wait_ge(turned_copied, b + 1)
                    for f in range(FB):
                        if f % 4 == 0:
                            pe.wait_ge(hidden_ready, b * FB)
                        for k in range(2):
                            last = pe.matmul(ps[:, 1 + f // 4, P * (f % 4):P * (f % 4) + P], weight1[:, k, f * P:f * P + P],
                                             cur_t[:, k, :], start=(k == 0), stop=(k == 1))
                        if f % 4 == 3:
                            last.then_inc(hidden_mult, 1)
                    pe.wait_ge(delta_ready, b * 2)
                    pe.matmul(ps[:, 3, 0:DIM], C.ones[0:1, :], bias2[:], start=True, stop=False)
                    for f in range(FB):
                        pe.wait_ge(hidden_ready, b * FB + f + 1)
                        last = pe.matmul(ps[:, 3, 0:DIM], hidden[:, f, :], weight2[:, f, :], start=False, stop=(f == FB - 1))
                    last.then_inc(mult_done, 1)

            @block.scalar
            def _(act):
                act.wait_ge(weights_in, loads)
                for b in repeated(act, NB):
                    act.wait_ge(turned, b + 1)
                    act.copy(cur_t[:], ps[:, 0, 0:2 * P].rearrange("p (k e) -> p k e", k=2)).then_inc(turned_copied, 1)
                    act.wait_ge(mult_done, b)
                    for f in range(FB):
                        if f % 4 == 0:
                            act.wait_ge(hidden_mult, b * 2 + f // 4 + 1)
                        act.activation(hidden[:, f, :], ps[:, 1 + f // 4, P * (f % 4):P * (f % 4) + P], ACT.Gelu,
                                       bias=bias1[:, f:f + 1]).then_inc(hidden_ready, 1)


def batch_norm(nc, C, label, agg, x, gamma_dram, beta_dram):
    ps = C.psum
    with phase(nc, label) as ph:
        square = ph.sbuf("square", [P, NB, DIM])
        valid = ph.sbuf("valid", [P, 1])
        vecs = ph.sbuf("vecs", [P, 2, DIM])
        mean = ph.sbuf("mean", [P, DIM])
        var = ph.sbuf("var", [P, DIM])
        root = ph.sbuf("root", [P, DIM])
        coef = ph.sbuf("coef", [P, 2, DIM])
        valid_set = ph.sem("valid_set")
        vecs_in = ph.sem("vecs_in")
        dve_step = ph.sem("dve_step")
        summed = ph.sem("summed")
        root_done = ph.sem("root_done")
        with ph.block() as block:
            @block.gpsimd
            def _(pool):
                pool.memset(valid[:], 1.0).then_inc(valid_set, 1)
                pool.wait_ge(valid_set, 1)
                pool.affine_select(out=valid[:], in_=valid[:], compare_op=ALU.is_gt, fill=0.0, base=LAST,
                                   pattern=[[0, 1]], channel_multiplier=-1).then_inc(valid_set, 1)

            @block.sync
            def _(sp):
                for i, v in enumerate((gamma_dram, beta_dram)):
                    sp.dma_start(vecs[:, i, :], v.rearrange("(o n) -> o n", o=1).to_broadcast([P, DIM])).then_inc(vecs_in, 16)

            @block.tensor
            def _(pe):
                for i, tile in enumerate((agg, square)):
                    pe.wait_ge(dve_step, (1, 5)[i])
                    for b in range(NB):
                        last = pe.matmul(ps[:, i, 0:DIM], C.ones[:], tile[:, b, :], start=(b == 0), stop=(b == NB - 1))
                    last.then_inc(summed, 1)

            @block.scalar
            def _(act):
                act.wait_ge(dve_step, 6)
                act.activation(root[:], var[:], ACT.Sqrt).then_inc(root_done, 1)

            @block.vector
            def _(dve):
                made = [0]

                def link(ins):
                    made[0] += 1
                    ins.then_inc(dve_step, 1)
                    dve.wait_ge(dve_step, made[0])

                last_block = agg[:, NB - 1, :]
                wide = lambda t: t.unsqueeze(1).to_broadcast([P, NB, DIM])
                dve.wait_ge(valid_set, 2)
                link(dve.tensor_scalar(last_block, last_block, valid[:], None, ALU.mult))
                dve.wait_ge(summed, 1)
                link(dve.tensor_scalar(mean[:], ps[:, 0, 0:DIM], 1.0 / N, None, ALU.mult))
                link(dve.tensor_tensor(agg[:], agg[:], wide(mean[:]), ALU.subtract))
                link(dve.tensor_scalar(last_block, last_block, valid[:], None, ALU.mult))
                link(dve.tensor_tensor(square[:], agg[:], agg[:], ALU.mult))
                dve.wait_ge(summed, 2)
                link(dve.tensor_scalar(var[:], ps[:, 1, 0:DIM], 1.0 / N, LN_EPS, ALU.mult, ALU.add))
                dve.wait_ge(root_done, 1)
                link(dve.reciprocal(coef[:, 0, :], root[:]))
                dve.wait_ge(vecs_in, 32)
                link(dve.tensor_tensor(coef[:, 1, :], coef[:, 0, :], vecs[:, 0, :], ALU.mult))
                link(dve.tensor_tensor(agg[:], agg[:], wide(coef[:, 1, :]), ALU.mult))
                link(dve.tensor_tensor(agg[:], agg[:], wide(vecs[:, 1, :]), ALU.add))
                dve.tensor_tensor(x[:], x[:], agg[:], ALU.add)


def load_x(nc, C, x_dram, x):
    with phase(nc, "load_x") as ph:
        cleared, loaded = ph.sem("cleared"), ph.sem("loaded")
        with ph.block() as block:
            @block.gpsimd
            def _(pool):
                pool.memset(x[:, NB - 1, :], 0.0).then_inc(cleared, 1)

            @block.sync
            def _(sp):
                full = (NB - 1) * P
                sp.dma_start(x[:, 0:NB - 1, :], x_dram[0:full].rearrange("(b p) w -> p b w", p=P)).then_inc(loaded, 16)
                sp.wait_ge(cleared, 1)
                sp.dma_start(x[0:LAST, NB - 1, :], x_dram[full:N]).then_inc(loaded, 16)
                sp.wait_ge(loaded, 32)


def store_out(nc, C, x, bias_dram, out):
    with phase(nc, "store_out") as ph:
        bias = ph.sbuf("bias", [P, DIM])
        bias_in, added, stored = ph.sem("bias_in"), ph.sem("added"), ph.sem("stored")
        with ph.block() as block:
            @block.vector
            def _(dve):
                dve.wait_ge(bias_in, 16)
                dve.tensor_tensor(x[:], x[:], bias[:].unsqueeze(1).to_broadcast([P, NB, DIM]), ALU.add).then_inc(added, 1)

            @block.sync
            def _(sp):
                full = (NB - 1) * P
                sp.dma_start(bias[:], bias_dram.rearrange("(o n) -> o n", o=1).to_broadcast([P, DIM])).then_inc(bias_in, 16)
                sp.wait_ge(added, 1)
                sp.dma_start(out[0:full].rearrange("(b p) w -> p b w", p=P), x[:, 0:NB - 1, :]).then_inc(stored, 16)
                sp.dma_start(out[full:N], x[0:LAST, NB - 1, :]).then_inc(stored, 16)
                sp.wait_ge(stored, 32)


def build(nc, A, out):
    with ExitStack() as ctx:
        C = make_constants(nc, ctx)
        by_src = make_order(nc, ctx, "by_src", 18, 24)
        by_dst = make_order(nc, ctx, "by_dst", 64, 64 + SPREAD + SPREAD_W)
        x = ctx.enter_context(nc.sbuf_tensor("x", [P, NB, DIM], F32))

        def table(name, rows, cols):
            return nc.dram_tensor(name, (rows, cols), F32, kind="Internal").ap()

        build_constants(nc, C)
        load_x(nc, C, A["x"], x)
        sort_edges(nc, C, by_src, "sort_src", A["src"], A["dst"], A["edge_attr_18"], None, None)
        sort_edges(nc, C, by_dst, "sort_dst", A["dst"], A["src"], A["edge_attr_64"], A["edge_type_8"], A["edge_weight"])

        H0 = 16
        q0, kv0 = table("q0", NR, P), table("kv0", NR, P + DIM)
        w = A["L0_gnn_Wqkv"]
        with nc.sbuf_tensor("h0", [P, NB, DIM], F32) as h:
            layer_norm(nc, C, "norm0", x, h)
            project(nc, C, "tables0", h, [(w, A["L0_gnn_bqkv"])],
                    [(0, P, (P // H0) ** -0.5), (P, 2 * P + DIM, 1.0)],
                    lambda rows, stage, sums: [(q0[rows, :], stage[:, 0:P]), (kv0[rows, :], stage[:, P:])])
        L = Layer(0, H0, by_src, P, P + DIM, P)
        C.sums = table("sums0", EP, L.out_width)
        edge_layer(nc, C, L, "edges0", (kv0, q0),
                   [(A["L0_gnn_Wk_rpe"], A["L0_gnn_bk_rpe"]), (A["L0_gnn_Wq_rpe"], A["L0_gnn_bq_rpe"])])
        combine(nc, C, L, "combine0", x, True)

        H1 = 8
        q1, kv1 = table("q1", NR, DIM), table("kv1", NR, 2 * DIM)
        with nc.sbuf_tensor("h1", [P, NB, DIM], F32) as h:
            layer_norm(nc, C, "norm1", x, h)
            with nc.sbuf_tensor("hn1", [P, NB, DIM], F32) as hn:
                layer_norm(nc, C, "norm1a", h, hn, (A["L1_gnn_ln1_g"], A["L1_gnn_ln1_b"]), relu=False)
                project(nc, C, "tables1", hn, [(A[f"L1_gnn_W{c}"], A[f"L1_gnn_b{c}"]) for c in "qkv"],
                        [(0, DIM, (DIM // H1) ** -0.5), (DIM, 2 * DIM, 1.0), (2 * DIM, 3 * DIM, 1.0)],
                        lambda rows, stage, sums: [(q1[rows, :], stage[:, 0:DIM]), (kv1[rows, :], stage[:, DIM:])])
            L = Layer(1, H1, by_dst, DIM, 2 * DIM, DIM)
            C.sums = table("sums1", EP, L.out_width)
            edge_layer(nc, C, L, "edges1", (kv1, q1), [(A["L1_gnn_We"], A["L1_gnn_be"])])
            with nc.sbuf_tensor("att1", [P, NB, DIM], F32) as att:
                combine(nc, C, L, "combine1", att, False)
                output_projection(nc, C, "out_proj1", att, h, A["L1_gnn_Wo"], A["L1_gnn_bo"], A["L1_gnn_alpha"])
                layer_norm(nc, C, "norm1b", h, att, (A["L1_gnn_ln2_g"], A["L1_gnn_ln2_b"]), relu=False)
                feed_forward(nc, C, "ff1", att, h, x, A["L1_gnn_W1"], A["L1_gnn_b1"], A["L1_gnn_W2"], A["L1_gnn_b2"],
                             A["L1_gnn_beta"])

        R = A["L2_gnn_weight"].shape[0]
        rel = table("rel2", NR * R, DIM)
        with nc.sbuf_tensor("h2", [P, NB, DIM], F32) as h:
            layer_norm(nc, C, "norm2", x, h)
            wide_rel = rel.rearrange("(n r) w -> n (r w)", r=R)
            project(nc, C, "tables2", h, [(A["L2_gnn_weight"][r], None) for r in range(R)],
                    [(c, c + 512, 1.0) for c in range(0, R * DIM, 512)],
                    lambda rows, stage, sums: [(wide_rel[rows, :], stage)])
        L = Layer(2, 0, by_dst, 0, DIM, 0)
        C.sums = table("sums2", EP, L.out_width)
        edge_layer(nc, C, L, "edges2", (rel,), [])
        with nc.sbuf_tensor("agg2", [P, NB, DIM], F32) as agg:
            combine(nc, C, L, "combine2", agg, False)
            batch_norm(nc, C, "batch_norm2", agg, x, A["L2_gnn_gamma"], A["L2_gnn_beta"])

        H3 = A["L3_gnn_attn_l"].shape[0]
        feat, right = table("feat3", NR, H3 + DIM), table("right3", NR, H3)
        with nc.sbuf_tensor("h3", [P, NB, DIM], F32) as h:
            layer_norm(nc, C, "norm3", x, h)
            project(nc, C, "tables3", h, [(A["L3_gnn_W"], None)], [(0, DIM, 1.0)],
                    lambda rows, stage, sums: [(feat[rows, H3:], stage), (feat[rows, 0:H3], sums[:, 0, :]), (right[rows, :], sums[:, 1, :])],
                    scores=((A["L3_gnn_attn_l"], A["L3_gnn_attn_r"]), H3))
        spread(nc, C, by_dst, "spread3", right)
        L = Layer(3, H3, by_dst, 0, H3 + DIM, H3)
        C.sums = table("sums3", EP, L.out_width)
        edge_layer(nc, C, L, "edges3", (feat,), [])
        combine(nc, C, L, "combine3", x, True)
        store_out(nc, C, x, A["L3_gnn_bias"], out)


_INS = ["x", "src", "dst", "edge_attr_18", "edge_attr_64", "edge_type_8", "edge_weight",
        "L0_gnn_Wqkv", "L0_gnn_bqkv", "L0_gnn_Wk_rpe", "L0_gnn_bk_rpe", "L0_gnn_Wq_rpe", "L0_gnn_bq_rpe",
        "L1_gnn_Wq", "L1_gnn_bq", "L1_gnn_Wk", "L1_gnn_bk", "L1_gnn_Wv", "L1_gnn_bv", "L1_gnn_We", "L1_gnn_be",
        "L1_gnn_Wo", "L1_gnn_bo", "L1_gnn_ln1_g", "L1_gnn_ln1_b", "L1_gnn_ln2_g", "L1_gnn_ln2_b",
        "L1_gnn_W1", "L1_gnn_b1", "L1_gnn_W2", "L1_gnn_b2", "L1_gnn_alpha", "L1_gnn_beta",
        "L2_gnn_weight", "L2_gnn_gamma", "L2_gnn_beta", "L3_gnn_W", "L3_gnn_attn_l", "L3_gnn_attn_r", "L3_gnn_bias"]


def kernel(**inputs):
    import numpy as _np
    import concourse.bacc as _bacc
    from concourse import mybir as _mybir
    from concourse.bass_utils import run_bass_kernel_spmd as _run

    nc = _bacc.Bacc("TRN2", target_bir_lowering=False, num_devices=1)
    arrays, args = {}, {}
    for name in _INS:
        a = _np.ascontiguousarray(inputs[name])
        arrays[f"in_{name}_dram"] = a
        args[name] = nc.dram_tensor(f"in_{name}_dram", a.shape, _mybir.dt.from_np(a.dtype), kind="ExternalInput").ap()
    out = nc.dram_tensor("out_dram", (N, DIM), F32, kind="ExternalOutput").ap()
    build(nc, args, out)
    r = _run(nc, [arrays], core_ids=[0])
    return r.results[0]["out_dram"]
```
